# Optimizing a Trainium2 kernel written in Bass

```python
import numpy as np
import jax
import jax.numpy as jnp

def _softmax(x, axis=-1):
    return jax.nn.softmax(x, axis=axis)

def _gelu(x):
    return jax.nn.gelu(x, approximate=True)

def _silu(x):
    return jax.nn.silu(x)

def _sigmoid(x):
    return jax.nn.sigmoid(x)

def _layernorm(x, axis=-1, eps=1e-05):
    m = jnp.mean(x, axis=axis, keepdims=True)
    v = jnp.var(x, axis=axis, keepdims=True)
    return (x - m) / jnp.sqrt(v + eps)

def _scatter_add(tgt, idx, src, axis=0):
    return tgt.at[idx].add(src)

def _segment_sum(src, seg, n):
    return jax.ops.segment_sum(src, seg, n)
kernel_name = 'mk_seq_postln_d1_jaxref_r4_1d5d1b'

def setup_inputs(seed: int=0):
    np.random.seed(seed)
    _w = jnp.asarray

    def _L0_attn_setup():
        import jax, jax.numpy as jnp
        import numpy as np
        B, T, D = (1, 512, 512)
        H, DK, DV, M = (16, 64, 128, 64)
        KEY_DIM, VALUE_DIM = (H * DK, H * DV)
        EPS = 1e-05
        CLAMP_MIN, CLAMP_MAX = (-32.0, 32.0)
        XAVIER_GAIN = 2.0 ** (-2.5)

        def _chunk_abc(q, k, v, s):
            scale = q.shape[-1] ** (-0.5)
            z = jax.lax.cumlogsumexp(s, axis=2)
            g = jnp.exp(jnp.concatenate([z[:, :, :1], z[:, :, :-1]], axis=2) - z)
            p = jnp.exp(s - z)
            tfirst = lambda x: jnp.moveaxis(x, 2, 0)
            qT, kT, vT, pT, gT = map(tfirst, (q * scale, k, v, p, g))
            b, h = (q.shape[0], q.shape[1])
            hk0 = jnp.zeros((b, h, q.shape[-1], s.shape[-1]), q.dtype)

            def step_k(hk, x):
                q_t, k_t, p_t, g_t = x
                hk = hk * g_t[:, :, None, :] + k_t[..., None] * p_t[:, :, None, :]
                return (hk, jnp.einsum('bhk,bhkm->bhm', q_t, hk))
            _, okT = jax.lax.scan(step_k, hk0, (qT, kT, pT, gT))
            pvT = jax.nn.softmax(okT, axis=-1)
            hv0 = jnp.zeros((b, h, s.shape[-1], v.shape[-1]), q.dtype)

            def step_v(hv, x):
                pv_t, v_t, p_t, g_t = x
                hv = hv * g_t[..., None] + p_t[..., None] * v_t[:, :, None, :]
                return (hv, jnp.einsum('bhm,bhmv->bhv', pv_t, hv))
            _, ovT = jax.lax.scan(step_v, hv0, (pvT, vT, pT, gT))
            return jnp.moveaxis(ovT, 0, 2)
        key = jax.random.key(seed)
        ks = jax.random.split(key, 8)

        def w(k, fan_in, fan_out):
            std = XAVIER_GAIN * np.sqrt(2.0 / (fan_in + fan_out))
            return jax.random.normal(k, (fan_in, fan_out), jnp.float32) * std
        return {'hidden_states': jax.random.normal(ks[0], (B, T, D), jnp.float32), 'Wq': w(ks[1], D, KEY_DIM), 'Wk': w(ks[2], D, KEY_DIM), 'Wv': w(ks[3], D, VALUE_DIM), 'Wg': w(ks[4], D, VALUE_DIM), 'Ws': w(ks[5], D, H * M), 'Wo': w(ks[6], VALUE_DIM, D), 'g_norm_weight': jnp.ones((DV,), jnp.float32)}
    _L0_attn_in = _L0_attn_setup()

    def _L0_ffn_setup():
        import jax, jax.numpy as jnp
        import numpy as np
        B, S, D, K, R = (4, 512, 512, 8, 64)
        key = jax.random.key(seed)
        ks = jax.random.split(key, 7)
        x = jax.random.normal(ks[0], (B, S, D), dtype=jnp.float32)
        U = jax.random.normal(ks[1], (K, D, R), dtype=jnp.float32) * 0.02
        V = jax.random.normal(ks[2], (K, R, D), dtype=jnp.float32) * 0.02
        W1 = jax.random.normal(ks[3], (D, D), dtype=jnp.float32) * 0.02
        b1 = jnp.zeros((D,), dtype=jnp.float32)
        W2 = jax.random.normal(ks[4], (D, K), dtype=jnp.float32) * 0.02
        b2 = jnp.zeros((K,), dtype=jnp.float32)
        return {'x': x, 'U': U, 'V': V, 'W1': W1, 'b1': b1, 'W2': W2, 'b2': b2}
    _L0_ffn_in = _L0_ffn_setup()
    _d = {'L0_attn_hidden_states': _L0_attn_in['hidden_states'], 'L0_attn_Wq': _L0_attn_in['Wq'], 'L0_attn_Wk': _L0_attn_in['Wk'], 'L0_attn_Wv': _L0_attn_in['Wv'], 'L0_attn_Wg': _L0_attn_in['Wg'], 'L0_attn_Ws': _L0_attn_in['Ws'], 'L0_attn_Wo': _L0_attn_in['Wo'], 'L0_attn_g_norm_weight': _L0_attn_in['g_norm_weight'], 'L0_ffn_U': _L0_ffn_in['U'], 'L0_ffn_V': _L0_ffn_in['V'], 'L0_ffn_W1': _L0_ffn_in['W1'], 'L0_ffn_b1': _L0_ffn_in['b1'], 'L0_ffn_W2': _L0_ffn_in['W2'], 'L0_ffn_b2': _L0_ffn_in['b2']}
    _x0 = _d['L0_attn_hidden_states']
    _d['L0_attn_hidden_states'] = jax.random.normal(jax.random.fold_in(jax.random.key(seed), 1), (4, 512, 512), dtype=_x0.dtype)
    del _x0
    return _d

def reference(L0_attn_hidden_states, L0_attn_Wq, L0_attn_Wk, L0_attn_Wv, L0_attn_Wg, L0_attn_Ws, L0_attn_Wo, L0_attn_g_norm_weight, L0_ffn_U, L0_ffn_V, L0_ffn_W1, L0_ffn_b1, L0_ffn_W2, L0_ffn_b2):

    def _L0_attn_ref(hidden_states, Wq, Wk, Wv, Wg, Ws, Wo, g_norm_weight):
        import jax, jax.numpy as jnp
        import numpy as np
        B, T, D = (1, 512, 512)
        H, DK, DV, M = (16, 64, 128, 64)
        KEY_DIM, VALUE_DIM = (H * DK, H * DV)
        EPS = 1e-05
        CLAMP_MIN, CLAMP_MAX = (-32.0, 32.0)
        XAVIER_GAIN = 2.0 ** (-2.5)

        def _chunk_abc(q, k, v, s):
            scale = q.shape[-1] ** (-0.5)
            z = jax.lax.cumlogsumexp(s, axis=2)
            g = jnp.exp(jnp.concatenate([z[:, :, :1], z[:, :, :-1]], axis=2) - z)
            p = jnp.exp(s - z)
            tfirst = lambda x: jnp.moveaxis(x, 2, 0)
            qT, kT, vT, pT, gT = map(tfirst, (q * scale, k, v, p, g))
            b, h = (q.shape[0], q.shape[1])
            hk0 = jnp.zeros((b, h, q.shape[-1], s.shape[-1]), q.dtype)

            def step_k(hk, x):
                q_t, k_t, p_t, g_t = x
                hk = hk * g_t[:, :, None, :] + k_t[..., None] * p_t[:, :, None, :]
                return (hk, jnp.einsum('bhk,bhkm->bhm', q_t, hk))
            _, okT = jax.lax.scan(step_k, hk0, (qT, kT, pT, gT))
            pvT = jax.nn.softmax(okT, axis=-1)
            hv0 = jnp.zeros((b, h, s.shape[-1], v.shape[-1]), q.dtype)

            def step_v(hv, x):
                pv_t, v_t, p_t, g_t = x
                hv = hv * g_t[..., None] + p_t[..., None] * v_t[:, :, None, :]
                return (hv, jnp.einsum('bhm,bhmv->bhv', pv_t, hv))
            _, ovT = jax.lax.scan(step_v, hv0, (pvT, vT, pT, gT))
            return jnp.moveaxis(ovT, 0, 2)
        b, t, _ = hidden_states.shape
        to_heads = lambda x, d: jnp.transpose(x.reshape(b, t, H, d), (0, 2, 1, 3))
        q = to_heads(hidden_states @ Wq, DK)
        k = to_heads(hidden_states @ Wk, DK)
        v = to_heads(hidden_states @ Wv, DV)
        s = jnp.clip(to_heads(hidden_states @ Ws, M), CLAMP_MIN, CLAMP_MAX)
        o = jnp.transpose(_chunk_abc(q, k, v, s), (0, 2, 1, 3))
        g = (hidden_states @ Wg).reshape(b, t, H, DV)
        o = o * jax.lax.rsqrt(jnp.mean(jnp.square(o), axis=-1, keepdims=True) + EPS) * g_norm_weight
        o = o * (g * jax.nn.sigmoid(g))
        return o.reshape(b, t, VALUE_DIM) @ Wo

    def _L0_ffn_ref(x, U, V, W1, b1, W2, b2):
        import jax, jax.numpy as jnp
        import numpy as np
        B, S, D, K, R = (4, 512, 512, 8, 64)
        h = jax.nn.relu(jnp.einsum('bsd,de->bse', x, W1) + b1)
        alpha = jax.nn.softmax(jnp.einsum('bse,ek->bsk', h, W2) + b2, axis=-1)
        vx = jnp.einsum('krd,bsd->bskr', V, x)
        uvx = jnp.einsum('kdr,bskr->bskd', U, vx)
        out = jnp.einsum('bsk,bskd->bsd', alpha, uvx)
        return out
    x = L0_attn_hidden_states
    x = _layernorm(x + _L0_attn_ref(x, L0_attn_Wq, L0_attn_Wk, L0_attn_Wv, L0_attn_Wg, L0_attn_Ws, L0_attn_Wo, L0_attn_g_norm_weight), axis=-1)
    x = _layernorm(x + _L0_ffn_ref(x, L0_ffn_U, L0_ffn_V, L0_ffn_W1, L0_ffn_b1, L0_ffn_W2, L0_ffn_b2), axis=-1)
    return x

_drawn_inputs = setup_inputs


def setup_inputs(seed=0):
    import zlib

    import numpy as np

    out = dict(_drawn_inputs(seed))
    spreads = {'L0_attn_g_norm_weight': (1.0, 0.6), 'L0_ffn_b1': (0.0, 0.8), 'L0_ffn_b2': (0.0, 0.8)}
    factors = {'L0_attn_Wq': 8.0,
     'L0_attn_Wk': 8.0,
     'L0_attn_Wv': 4.831,
     'L0_attn_Wg': 4.809,
     'L0_attn_Ws': 8.0,
     'L0_attn_Wo': 4.804,
     'L0_ffn_W1': 8.0,
     'L0_ffn_W2': 8.0}
    for name, (base, spread) in spreads.items():
        noise = np.random.default_rng([zlib.crc32(name.encode()), seed]).standard_normal(out[name].shape)
        drawn = base * np.exp(spread * noise) if base else spread * noise
        out[name] = jnp.asarray(drawn.astype(out[name].dtype))
    for name, factor in factors.items():
        out[name] = (out[name] * factor).astype(out[name].dtype)
    return out
```

```python
from contextlib import ExitStack

import concourse.bass as bass
from concourse import mybir
from concourse.alu_op_type import AluOpType as ALU

ACT = mybir.ActivationFunctionType
F32 = mybir.dt.float32
F32R = mybir.dt.float32r
AX_X = mybir.AxisListType.X

P = 128
BANK = 512

B, T, D = 4, 512, 512
H, DK, DV, M = 16, 64, 128, 64
R_KEEP, K_EXP, R_EXP = 128, 8, 64
CLAMP = 32.0
EPS = 1e-5

KT = D // P
PAIRS = H // 2
CH = T // P
CELLS = PAIRS * B
VW = 2 * DV
NT = B * CH


class Cell:

    def __init__(self, j, b):
        self.j, self.b = j, b

    def shifted(self, by):
        return Cell(self.j, self.b + by)

    @property
    def batch(self):
        return self.b % B

    def count(self, per_cell, k=0):
        fixed = per_cell * self.b + k
        return fixed if self.j is None else self.j * (per_cell * B) + fixed


P_USES = ["vg0", "vg1", "wo0", "wo1", "wo2", "wo3", "vg2", "vg3", "s", "q", "k"]
T_USES = ["e", "k", "rz", "y0", "y1", "pz"]


def turn(cell, use, uses, start):
    def order(number):
        if number == 0:
            return [u for u in uses if u[:2] != "wo" and u[0] != "y"]
        if number == CELLS:
            return [u for u in uses if u[:2] == "wo" or u[0] == "y"]
        if number == CELLS - 1 and uses is P_USES:
            return [u for u in uses if u not in ("s", "q", "k")]
        return uses

    line = [(-1, u) for u in start]
    line += [(n, u) for n in range(cell.b + 1) for u in order(n)]
    at = line.index((cell.b, use))
    n, before = line[at - 2] if at >= 2 else (None, None)
    return at % 2, None if n is None else (cell.shifted(n - cell.b), before)


def p_turn(cell, use):
    return turn(cell, use, P_USES, ["s", "q", "k"])


def t_turn(cell, use):
    return turn(cell, use, T_USES, [])


def build(nc, x, Wq, Wk, Wv, Wg, Ws, Wo, g_norm, U, V, W1, b1, W2, b2, out):
    with ExitStack() as whole:
        acc = whole.enter_context(nc.sbuf_tensor("acc", [P, NT, D], F32))
        ident = whole.enter_context(nc.sbuf_tensor("ident", [P, P], F32))
        attention(nc, acc, ident, x, Wq, Wk, Wv, Wg, Ws, Wo, g_norm)
        experts(nc, acc, ident, U, V, W1, b1, W2, b2, out)


def attention(nc, acc, ident, x, Wq, Wk, Wv, Wg, Ws, Wo, g_norm):
    ctx = ExitStack()
    with ctx:
        def sb(name, shape, dt=F32):
            return ctx.enter_context(nc.sbuf_tensor(name, shape, dt))

        def bank(name):
            return ctx.enter_context(nc.psum_tensor(name, [P, BANK], F32))

        def sem(name):
            return ctx.enter_context(nc.semaphore(name))

        xt_hi = sb("xt_hi", [P, KT, B, T], F32R)
        xt_lo = sb("xt_lo", [P, KT, B, T], F32R)
        wsqk_hi = sb("wsqk_hi", [P, 3, KT, P], F32R)
        wsqk_lo = sb("wsqk_lo", [P, 3, KT, P], F32R)
        wvg_hi = sb("wvg_hi", [P, KT, 2 * VW], F32R)
        wvg_lo = sb("wvg_lo", [P, KT, 2 * VW], F32R)
        wo_hi = sb("wo_hi", [P, 2, D], F32R)
        wo_lo = sb("wo_lo", [P, 2, D], F32R)
        raw = sb("raw", [P, 3, BANK])
        e_t = sb("e_t", [P, 2, T])
        rz_t = sb("rz_t", [P, T])
        q_t = sb("q_t", [P, T])
        q_bd = sb("q_bd", [P, 2, T])
        k_t = sb("k_t", [P, T])
        e_tok = sb("e_tok", [P, CH, 4, M])
        k_tok = sb("k_tok", [P, CH, P])
        rz_tok = sb("rz_tok", [P, CH, P])
        w_t = sb("w_t", [P, CH, 2, P])
        hk = sb("hk", [P, CH - 1, P])
        hv = sb("hv", [P, CH - 1, VW])
        ok = sb("ok", [P, CH, 2, M])
        pz = sb("pz", [P, CH, 2, M])
        pz_t = sb("pz_t", [P, T])
        pz_bd = sb("pz_bd", [P, 2, T])
        v_tok = sb("v_tok", [P, CH, VW])
        gate = sb("gate", [P, CH, VW])
        th = sb("th", [P, 2, VW])
        y = sb("y", [P, CH, 2, DV])
        yt_hi = sb("yt_hi", [P, 2, 2, 2, P], F32R)
        yt_lo = sb("yt_lo", [P, 2, 2, 2, P], F32R)
        causal = sb("causal", [P, P])
        own = sb("own", [P, 2, DV])
        gn = sb("gn", [P, 2])
        top = sb("top", [P, 2 * CH])
        esum = sb("esum", [P, 2 * CH])
        esq = sb("esq", [P, 2 * CH])
        osq = sb("osq", [P, 2 * CH])
        ovar = sb("ovar", [P, 2 * CH])
        orstd = sb("orstd", [P, 2 * CH])
        minus_half = sb("minus_half", [P, 2 * CH])

        PB = [bank("p0"), bank("p1")]
        TB = [bank("t0"), bank("t1")]
        SB = [bank("s0"), bank("s1")]
        OB = bank("o")
        XB = bank("xb")

        x_in = [sem(f"x_in{b}") for b in range(B)]
        raw_in = [sem(f"raw_in{i}") for i in range(3)]
        gn_in = sem("gn_in")
        w_hi_done = sem("w_hi_done")
        w_lo_done = sem("w_lo_done")
        wo_hi_done = sem("wo_hi_done")
        wo_lo_done = sem("wo_lo_done")
        const_done = sem("const_done")
        own_done = sem("own_done")
        gn_half = sem("gn_half")
        xt_turned = sem("xt_turned")
        xt_hi_done = sem("xt_hi_done")
        xt_lo_done = sem("xt_lo_done")
        s_proj, q_proj, k_proj, vg_proj = sem("s_proj"), sem("q_proj"), sem("k_proj"), sem("vg_proj")
        e_turned, k_turned, rz_turned = sem("e_turned"), sem("k_turned"), sem("rz_turned")
        y_turned, pz_turned = sem("y_turned"), sem("pz_turned")
        scores = sem("scores")
        hk_summed, ok_summed, hv_summed = sem("hk_summed"), sem("ok_summed"), sem("hv_summed")
        weights, values, rows = sem("weights"), sem("values"), sem("rows")
        s_clipped, e_done, z_done, rz_done = sem("s_clipped"), sem("e_done"), sem("z_done"), sem("rz_done")
        q_done, k_done, v_done, th_done, gate_done = (
            sem("q_done"), sem("k_done"), sem("v_done"), sem("th_done"), sem("gate_done"))
        e_tok_done, k_tok_done, rz_tok_done = sem("e_tok_done"), sem("k_tok_done"), sem("rz_tok_done")
        scores_masked, weights_masked = sem("scores_masked"), sem("weights_masked")
        hk_kept, hv_kept = sem("hk_kept"), sem("hv_kept")
        ok_scaled, top_done, ok_less_top, exp_done = (
            sem("ok_scaled"), sem("top_done"), sem("ok_less_top"), sem("exp_done"))
        pz_done, esum_done, esq_done = sem("pz_done"), sem("esum_done"), sem("esq_done")
        pz_t_done = sem("pz_t_done")
        osq_done, ovar_done, orstd_done = sem("osq_done"), sem("ovar_done"), sem("orstd_done")
        y_done, yt_hi_done, yt_lo_done = sem("y_done"), sem("yt_hi_done"), sem("yt_lo_done")
        added = sem("added")

        def tokens(c):
            return slice(c * P, (c + 1) * P)

        def load_piece(sp, J, name, i):
            slot = raw[:, i % 3, :]
            if name == "sqk":
                w = (Ws, Wq, Wk)[i]
                src = w.rearrange("(k p) n -> p k n", p=P)[:, :, bass.ds(J * P, P)]
                sp.dma_start(slot.rearrange("p (k n) -> p k n", k=KT), src).then_inc(raw_in[i % 3], 16)
            elif name == "vg":
                kt = i - 3
                for half, w in ((0, Wv), (1, Wg)):
                    src = w[kt * P:(kt + 1) * P, bass.ds(J * VW, VW)]
                    sp.dma_start(slot[:, half * VW:(half + 1) * VW], src).then_inc(raw_in[i % 3], 16)
            else:
                h = i - 7
                src = Wo[bass.ds(J * VW + h * DV, DV), :]
                sp.dma_start(slot, src).then_inc(raw_in[i % 3], 16)

        LANDED = {0: (0, 1), 3: (0, 3), 6: (0, 5), 1: (1, 1), 4: (1, 3), 7: (1, 4), 2: (2, 1), 5: (2, 3), 8: (2, 4)}
        PER_PAIR = (5, 4, 4)

        def wait_landed(eng, J, i):
            slot, k = LANDED[i]
            eng.wait_ge(raw_in[slot], J * (16 * PER_PAIR[slot]) + 16 * k)

        def name_of(i):
            return "sqk" if i < 3 else "vg" if i < 7 else "wo"

        def part(i, which):
            if i < 3:
                return (wsqk_hi, wsqk_lo)[which][:, i, :, :].rearrange("p k n -> p (k n)")
            if i < 7:
                return (wvg_hi, wvg_lo)[which][:, i - 3, :]
            return (wo_hi, wo_lo)[which][:, i - 7, :]

        def first(cell):
            return cell.j is None and cell.b == 0

        block = ctx.enter_context(nc.Block())

        @block.sync
        def _(sp):
            sp.dma_start(gn[:, 0:1], g_norm.rearrange("(p a) -> p a", a=1)).then_inc(gn_in, 16)
            xv = x.rearrange("b (n p) d -> b p n d", p=P)
            for i in range(3):
                load_piece(sp, 0, name_of(i), i)
            for b in range(B):
                sp.dma_start(acc[:, b * CH:(b + 1) * CH, :], xv[b]).then_inc(x_in[b], 16)
            for i in range(3, 9):
                sp.wait_ge(w_lo_done, i - 2)
                load_piece(sp, 0, name_of(i), i)
            with sp.Fori(1, PAIRS) as J:
                for i in range(9):
                    if i == 0:
                        sp.wait_ge(w_lo_done, J * 7)
                    elif i < 3:
                        sp.wait_ge(wo_lo_done, J * 2 + (i - 2))
                    else:
                        sp.wait_ge(w_lo_done, J * 7 + (i - 2))
                    load_piece(sp, J, name_of(i), i)

        def split_low(pool, J, i, cell):
            pool.wait_ge(w_hi_done, J * 7 + (i + 1))
            nc.gpsimd.tensor_tensor(part(i, 1), raw[:, i % 3, :], part(i, 0).bitcast(F32),
                                    ALU.subtract).then_inc(w_lo_done, 1)

        def cell_gpsimd(pool, cell, J=None):
            if J is not None:
                for i in range(7):
                    split_low(pool, J, i, cell)
            pool.wait_ge(ovar_done, cell.count(1, 1))
            nc.gpsimd.tensor_tensor(orstd[:], ovar[:], minus_half[:], ALU.pow).then_inc(orstd_done, 1)

        @block.gpsimd
        def _(pool):
            nc.gpsimd.memset(ident[:], 0.0).then_inc(const_done, 1)
            nc.gpsimd.memset(causal[:], 1.0).then_inc(const_done, 1)
            nc.gpsimd.memset(minus_half[:], -0.5).then_inc(const_done, 1)
            pool.wait_ge(const_done, 3)
            nc.gpsimd.affine_select(out=ident[:], in_=ident[:], compare_op=ALU.not_equal, fill=1.0, base=0,
                                    pattern=[[-1, P]], channel_multiplier=1).then_inc(const_done, 1)
            nc.gpsimd.affine_select(out=causal[:], in_=causal[:], compare_op=ALU.is_ge, fill=0.0, base=0,
                                    pattern=[[1, P]], channel_multiplier=-1).then_inc(const_done, 1)
            for i in range(7):
                split_low(pool, 0, i, None)
            cell_gpsimd(pool, Cell(None, 0))
            with pool.Fori(0, PAIRS - 1) as j:
                for b in range(1, B + 1):
                    cell_gpsimd(pool, Cell(j, b), j + 1 if b == 3 else None)
            for b in range(1, B):
                cell_gpsimd(pool, Cell(None, B * (PAIRS - 1) + b))

        def split_high(act, J, i, release):
            wait_landed(act, J, i)
            if release is not None:
                act.wait_ge(*release)
            if i < 7:
                nc.scalar.activation(part(i, 0), raw[:, i % 3, :], ACT.Copy).then_inc(w_hi_done, 1)
            else:
                nc.scalar.activation(part(i, 0), raw[:, i % 3, :], ACT.Copy,
                                     scale=gn[:, 1:2]).then_inc(wo_hi_done, 1)

        def slots_scalar(act, m):
            act.wait_ge(s_clipped, m.count(1, 1))
            e = e_t[:, m.b % 2, :]
            nc.scalar.activation(e, e, ACT.Exp).then_inc(e_done, 1)

        def queries_scalar(act, m):
            bk, _ = p_turn(m.shifted(-1), "q")
            ps = PB[bk]
            act.wait_ge(q_proj, m.count(1, 1))
            scale = float(DK) ** -0.5
            nc.scalar.activation(q_t[:], ps[:], ACT.Copy, scale=scale)
            nc.scalar.activation(q_bd[0:DK, 0, :], ps[0:DK, :], ACT.Copy, scale=scale)
            nc.scalar.activation(q_bd[DK:P, 1, :], ps[DK:P, :], ACT.Copy, scale=scale).then_inc(q_done, 1)

        def keys_scalar(act, m):
            bk, _ = p_turn(m.shifted(-1), "k")
            act.wait_ge(k_proj, m.count(1, 1))
            nc.scalar.activation(k_t[:], PB[bk][:], ACT.Copy).then_inc(k_done, 1)

        def values_scalar(act, cell, c):
            bk, _ = p_turn(cell, f"vg{c}")
            act.wait_ge(vg_proj, cell.count(CH, c + 1))
            nc.scalar.activation(v_tok[:, c, :], PB[bk][:, 0:VW], ACT.Copy).then_inc(v_done, 1)
            if c >= 2 or not first(cell):
                act.wait_ge(gate_done, cell.count(CH, c - 1))
            nc.scalar.activation(th[:, c % 2, :], PB[bk][:, VW:2 * VW], ACT.Tanh,
                                 scale=0.5).then_inc(th_done, 1)

        def y_high(act, cell, half):
            prev = cell.shifted(-1)
            bk, _ = t_turn(cell, f"y{half}")
            act.wait_ge(y_turned, prev.count(2, half + 1))
            nc.scalar.activation(yt_hi[:, half, :, :, :].rearrange("p c h t -> p (c h t)"), TB[bk][:],
                                 ACT.Copy).then_inc(yt_hi_done, 1)

        def cell_scalar(act, cell, J=None, wo_J=None, last=False):
            nxt = cell.shifted(1)
            bk, _ = t_turn(cell, "e")
            act.wait_ge(e_turned, cell.count(1, 1))
            nc.scalar.activation(e_tok[:, :, 1:3, :], TB[bk][:].rearrange("p (c h m) -> p c h m", c=CH, h=2),
                                 ACT.Copy).then_inc(e_tok_done, 1)
            bk, _ = t_turn(cell, "k")
            act.wait_ge(k_turned, cell.count(1, 1))
            nc.scalar.activation(k_tok[:].rearrange("p c n -> p (c n)"), TB[bk][:], ACT.Copy).then_inc(k_tok_done, 1)
            bk, _ = t_turn(cell, "rz")
            act.wait_ge(rz_turned, cell.count(1, 1))
            nc.scalar.activation(rz_tok[:].rearrange("p c n -> p (c n)"), TB[bk][:], ACT.Copy).then_inc(rz_tok_done, 1)
            if J is not None:
                for i, used in ((0, s_proj), (1, q_proj), (2, k_proj)):
                    split_high(act, J, i, (used, J * B))
            values_scalar(act, cell, 0)
            values_scalar(act, cell, 1)
            if not first(cell):
                y_high(act, cell, 0)
                y_high(act, cell, 1)
            act.wait_ge(ok_less_top, cell.count(1, 1))
            flat = ok[:].rearrange("p c h m -> p (c h m)")
            nc.scalar.activation(flat, flat, ACT.Exp).then_inc(exp_done, 1)
            values_scalar(act, cell, 2)
            bk, _ = t_turn(cell, "pz")
            act.wait_ge(pz_turned, cell.count(1, 1))
            nc.scalar.activation(pz_t[:], TB[bk][:], ACT.Copy)
            nc.scalar.activation(pz_bd[0:M, 0, :], TB[bk][0:M, :], ACT.Copy)
            nc.scalar.activation(pz_bd[M:P, 1, :], TB[bk][M:P, :], ACT.Copy).then_inc(pz_t_done, 1)
            values_scalar(act, cell, 3)
            if J is not None:
                for i in range(3, 7):
                    split_high(act, J, i, (vg_proj, J * (B * CH)))
            if not last:
                slots_scalar(act, nxt)
                queries_scalar(act, nxt)
                keys_scalar(act, nxt)
            if wo_J is not None:
                for i in (7, 8):
                    split_high(act, wo_J, i, (rows, wo_J * (B * CH)))
            for half in range(2):
                ps = (OB, SB[0])[half]
                act.wait_ge(values, cell.count(2, half + 1))
                for c in range(2):
                    for h in range(2):
                        g = (2 * half + c) * 2 + h
                        nc.scalar.activation(y[:, 2 * half + c, h, :], ps[:, (2 * c + h) * DV:(2 * c + h + 1) * DV],
                                             ACT.Square, accum_out=osq[:, g:g + 1]).then_inc(osq_done, 1)

        @block.scalar
        def _(act):
            act.wait_ge(gn_in, 16)
            nc.scalar.activation(gn[:, 1:2], gn[:, 0:1], ACT.Copy, scale=0.5).then_inc(gn_half, 1)
            for i in range(3):
                split_high(act, 0, i, None)
            for g in range(B * KT):
                act.wait_ge(xt_turned, g + 1)
                nc.scalar.activation(xt_hi[:, g % KT, g // KT, :], SB[g % 2][:], ACT.Copy).then_inc(xt_hi_done, 1)
            for i in range(3, 7):
                split_high(act, 0, i, None)
            act.wait_ge(gn_half, 1)
            for i in (7, 8):
                split_high(act, 0, i, None)
            slots_scalar(act, Cell(None, 0))
            queries_scalar(act, Cell(None, 0))
            keys_scalar(act, Cell(None, 0))
            cell_scalar(act, Cell(None, 0))
            with act.Fori(0, PAIRS - 1) as j:
                for b in range(1, B + 1):
                    cell_scalar(act, Cell(j, b), j + 1 if b == 3 else None, j + 1 if b == 4 else None)
            for b in range(1, B):
                cell_scalar(act, Cell(None, B * (PAIRS - 1) + b), last=b == B - 1)
            y_high(act, Cell(None, CELLS), 0)
            y_high(act, Cell(None, CELLS), 1)

        def slots_vector(dve, m):
            bk, _ = p_turn(m.shifted(-1), "s")
            dve.wait_ge(s_proj, m.count(1, 1))
            nc.vector.tensor_scalar(e_t[:, m.b % 2, :], PB[bk][:], -CLAMP, CLAMP, ALU.max,
                                    ALU.min).then_inc(s_clipped, 1)

        def sums_vector(dve, m):
            dve.wait_ge(e_done, m.count(1, 1))
            e = e_t[:, m.b % 2, :]
            nc.vector.tensor_tensor_scan(rz_t[:], e, e, 0.0, ALU.add, ALU.bypass).then_inc(z_done, 1)

        def inverse_vector(dve, m):
            dve.wait_ge(z_done, m.count(1, 1))
            nc.vector.reciprocal(rz_t[:], rz_t[:]).then_inc(rz_done, 1)

        def masked(dve, cell, half, ready, done):
            dve.wait_ge(ready, cell.count(2, half + 1))
            nc.vector.tensor_tensor(
                w_t[:, 2 * half:2 * half + 2, :, :].rearrange("p c h t -> p (c h) t"),
                SB[half][:].rearrange("p (a t) -> p a t", a=4),
                causal[:].rearrange("p (a t) -> p a t", a=1).broadcast_to([P, 4, P]),
                ALU.mult).then_inc(done, 1)

        def gate_vector(dve, cell, c):
            bk, _ = p_turn(cell, f"vg{c}")
            dve.wait_ge(th_done, cell.count(CH, c + 1))
            if c == 0 and not first(cell):
                dve.wait_ge(y_done, cell.count(2 * CH, 0))
            nc.vector.scalar_tensor_tensor(out=gate[:, c, :], in0=th[:, c % 2, :], scalar=1.0,
                                           in1=PB[bk][:, VW:2 * VW], op0=ALU.add,
                                           op1=ALU.mult).then_inc(gate_done, 1)

        def y_vector(dve, prev):
            dve.wait_ge(orstd_done, prev.count(1, 1))
            dve.wait_ge(gate_done, prev.count(CH, CH))
            for half in range(2):
                ps = (OB, SB[0])[half]
                for c in range(2):
                    for h in range(2):
                        g = (2 * half + c) * 2 + h
                        nc.vector.scalar_tensor_tensor(
                            out=y[:, 2 * half + c, h, :], in0=ps[:, (2 * c + h) * DV:(2 * c + h + 1) * DV],
                            scalar=orstd[:, g:g + 1], in1=gate[:, 2 * half + c, h * DV:(h + 1) * DV],
                            op0=ALU.mult, op1=ALU.mult).then_inc(y_done, 1)

        def y_low(dve, cell, half):
            prev = cell.shifted(-1)
            bk, _ = t_turn(cell, f"y{half}")
            dve.wait_ge(yt_hi_done, prev.count(2, half + 1))
            nc.vector.tensor_tensor(yt_lo[:, half, :, :, :].rearrange("p c h t -> p (c h t)"), TB[bk][:],
                                    yt_hi[:, half, :, :, :].rearrange("p c h t -> p (c h t)").bitcast(F32),
                                    ALU.subtract).then_inc(yt_lo_done, 1)

        def kept(dve, cell, c, summed, done, dst, src, rows_own):
            dve.wait_ge(summed, cell.count(CH - 1, c + 1))
            nc.vector.tensor_tensor(dst, src, rows_own, ALU.mult).then_inc(done, 1)

        def add_rows(dve, cell, c):
            prev = cell.shifted(-1)
            bk, _ = p_turn(cell, f"wo{c}")
            a = acc[:, prev.batch * CH + c, :]
            dve.wait_ge(rows, prev.count(CH, c + 1))
            nc.vector.tensor_tensor(a, PB[bk][:], a, ALU.add).then_inc(added, 1)

        def low_rows(dve, J):
            for i in (7, 8):
                dve.wait_ge(wo_hi_done, J * 2 + (i - 6))
                nc.vector.scalar_tensor_tensor(out=part(i, 1), in0=raw[:, i % 3, :], scalar=gn[:, 1:2],
                                               in1=part(i, 0).bitcast(F32), op0=ALU.mult,
                                               op1=ALU.subtract).then_inc(wo_lo_done, 1)

        def cell_vector(dve, cell, wo_J=None, last=False):
            nxt = cell.shifted(1)
            if not first(cell):
                y_vector(dve, cell.shifted(-1))
            gate_vector(dve, cell, 0)
            gate_vector(dve, cell, 1)
            masked(dve, cell, 0, scores, scores_masked)
            masked(dve, cell, 1, scores, scores_masked)
            if not first(cell):
                y_low(dve, cell, 0)
                y_low(dve, cell, 1)
            for c in range(CH - 1):
                kept(dve, cell, c, hk_summed, hk_kept, hk[:, c, :], XB[:, 0:P],
                     own[:, :, 0:M])
            flat = ok[:].rearrange("p c h m -> p (c h m)")
            groups = ok[:].rearrange("p c h m -> p (c h) m")
            dve.wait_ge(ok_summed, cell.count(1, 1))
            dve.wait_ge(rz_tok_done, cell.count(1, 1))
            nc.vector.tensor_tensor(flat, OB[:], rz_tok[:].rearrange("p c n -> p (c n)"),
                                    ALU.mult).then_inc(ok_scaled, 1)
            dve.wait_ge(ok_scaled, cell.count(1, 1))
            nc.vector.tensor_reduce(top[:], groups, AX_X, ALU.max).then_inc(top_done, 1)
            dve.wait_ge(top_done, cell.count(1, 1))
            nc.vector.tensor_tensor(groups, groups,
                                    top[:].rearrange("p (g a) -> p g a", a=1).broadcast_to([P, 2 * CH, M]),
                                    ALU.subtract).then_inc(ok_less_top, 1)
            if not first(cell):
                add_rows(dve, cell, 0)
            dve.wait_ge(exp_done, cell.count(1, 1))
            nc.vector.tensor_tensor(pz[:].rearrange("p c h m -> p (c h m)"), flat,
                                    rz_tok[:].rearrange("p c n -> p (c n)"), ALU.mult).then_inc(pz_done, 1)
            if not first(cell):
                add_rows(dve, cell, 1)
            nc.vector.tensor_reduce(esum[:], groups, AX_X, ALU.add).then_inc(esum_done, 1)
            dve.wait_ge(esum_done, cell.count(1, 1))
            nc.vector.scalar_tensor_tensor(out=esq[:], in0=esum[:], scalar=EPS, in1=esum[:], op0=ALU.mult,
                                           op1=ALU.mult).then_inc(esq_done, 1)
            if not first(cell):
                add_rows(dve, cell, 2)
                add_rows(dve, cell, 3)
            for c in range(CH - 1):
                kept(dve, cell, c, hv_summed, hv_kept, hv[:, c, :], XB[:, P:P + VW],
                     own[:].rearrange("p h n -> p (h n)"))
                if c < 2:
                    gate_vector(dve, cell, c + 2)
            if not last:
                slots_vector(dve, nxt)
                sums_vector(dve, nxt)
            masked(dve, cell, 0, weights, weights_masked)
            masked(dve, cell, 1, weights, weights_masked)
            if not last:
                inverse_vector(dve, nxt)
            if wo_J is not None:
                low_rows(dve, wo_J)
            dve.wait_ge(osq_done, cell.count(2 * CH, 2 * CH))
            dve.wait_ge(esq_done, cell.count(1, 1))
            nc.vector.scalar_tensor_tensor(out=ovar[:], in0=osq[:], scalar=1.0 / DV, in1=esq[:], op0=ALU.mult,
                                           op1=ALU.add).then_inc(ovar_done, 1)

        @block.vector
        def _(dve):
            nc.vector.memset(own[:], 0.0).then_inc(own_done, 1)
            nc.vector.memset(q_bd[:], 0.0).then_inc(own_done, 1)
            nc.vector.memset(pz_bd[:], 0.0).then_inc(own_done, 1)
            nc.vector.memset(e_tok[:], 0.0).then_inc(own_done, 1)
            dve.wait_ge(own_done, 4)
            nc.vector.memset(own[0:M, 0, :], 1.0).then_inc(own_done, 1)
            nc.vector.memset(own[M:P, 1, :], 1.0).then_inc(own_done, 1)
            for g in range(B * KT):
                dve.wait_ge(xt_hi_done, g + 1)
                nc.vector.tensor_tensor(xt_lo[:, g % KT, g // KT, :], SB[g % 2][:],
                                        xt_hi[:, g % KT, g // KT, :].bitcast(F32),
                                        ALU.subtract).then_inc(xt_lo_done, 1)
            dve.wait_ge(gn_half, 1)
            low_rows(dve, 0)
            dve.wait_ge(const_done, 5)
            dve.wait_ge(own_done, 6)
            m = Cell(None, 0)
            slots_vector(dve, m)
            sums_vector(dve, m)
            inverse_vector(dve, m)
            cell_vector(dve, m)
            with dve.Fori(0, PAIRS - 1) as j:
                for b in range(1, B + 1):
                    cell_vector(dve, Cell(j, b), j + 1 if b == 4 else None)
            for b in range(1, B):
                cell_vector(dve, Cell(None, B * (PAIRS - 1) + b), last=b == B - 1)
            tail = Cell(None, CELLS)
            y_vector(dve, tail.shifted(-1))
            y_low(dve, tail, 0)
            y_low(dve, tail, 1)
            for c in range(CH):
                add_rows(dve, tail, c)

        p_read = {"s": (s_clipped, 1, 2), "q": (q_done, 1, 2), "k": (k_done, 1, 2)}
        t_read = {"e": (e_tok_done, 1, 1), "k": (k_tok_done, 1, 1), "rz": (rz_tok_done, 1, 1), "pz": (pz_t_done, 1, 1)}
        for c in range(CH):
            p_read[f"vg{c}"] = (gate_done, CH, c + 1)
            p_read[f"wo{c}"] = (added, CH, c + 1 - CH)
        for half in range(2):
            t_read[f"y{half}"] = (yt_lo_done, 2, half - 1)

        def wait_read(pe, read, before):
            if before is not None:
                its_cell, use = before
                done, per_cell, k = read[use]
                pe.wait_ge(done, its_cell.count(per_cell, k))

        def split_product(out_, terms, done=None):
            n = len(terms)
            for k, ((lh, ll), (rh, rl)) in enumerate(terms):
                nc.tensor.matmul(out_, lh, rh, start=(k == 0), stop=False)
                nc.tensor.matmul(out_, lh, rl, start=False, stop=False)
                last = nc.tensor.matmul(out_, ll, rh, start=False, stop=(k == n - 1))
            last.then_inc(done, 1)

        def feature_proj(pe, m, i, done):
            bk, before = p_turn(m.shifted(-1), "sqk"[i])
            wait_read(pe, p_read, before)
            if first(m):
                pe.wait_ge(w_lo_done, i + 1)
            elif m.j is not None and m.b == B:
                pe.wait_ge(w_lo_done, (m.j + 1) * 7 + (i + 1))
            b = m.batch
            split_product(PB[bk][:], [((wsqk_hi[:, i, kt, :], wsqk_lo[:, i, kt, :]),
                                       (xt_hi[:, kt, b, :], xt_lo[:, kt, b, :])) for kt in range(KT)], done)

        def token_proj(pe, cell, c):
            bk, before = p_turn(cell, f"vg{c}")
            wait_read(pe, p_read, before)
            if c == 0 and first(cell):
                pe.wait_ge(w_lo_done, 7)
            if c == 0 and cell.j is not None and cell.b == B:
                pe.wait_ge(w_lo_done, (cell.j + 1) * 7 + 7)
            t = tokens(c)
            b = cell.batch
            split_product(PB[bk][:], [((xt_hi[:, kt, b, t], xt_lo[:, kt, b, t]),
                                       (wvg_hi[:, kt, :], wvg_lo[:, kt, :])) for kt in range(KT)], vg_proj)

        def turned(pe, cell, use, blocks, done):
            bk, before = t_turn(cell, use)
            wait_read(pe, t_read, before)
            for i, blk in enumerate(blocks):
                last = nc.tensor.transpose(TB[bk][:, i * P:(i + 1) * P], blk, ident[:])
            last.then_inc(done, 1)

        def output_rows(pe, cell, c):
            prev = cell.shifted(-1)
            bk, before = p_turn(cell, f"wo{c}")
            wait_read(pe, p_read, before)
            pe.wait_ge(yt_lo_done, prev.count(2, c // 2 + 1))
            if c == 0:
                if cell.j is not None and cell.b == 1:
                    pe.wait_ge(wo_lo_done, cell.j * 2 + 2)
                elif cell.j is None and cell.b == CELLS - B + 1:
                    pe.wait_ge(wo_lo_done, 2 * PAIRS)
            split_product(PB[bk][:], [((yt_hi[:, c // 2, c % 2, h, :], yt_lo[:, c // 2, c % 2, h, :]),
                                       (wo_hi[:, h, :], wo_lo[:, h, :])) for h in range(2)], rows)

        def pair_blocks(pe, half, lhs, rhs, done):
            for c in (2 * half, 2 * half + 1):
                last = nc.tensor.matmul(SB[half][:, (c % 2) * 2 * P:(c % 2 + 1) * 2 * P].rearrange("p (h t) -> p h t", h=2),
                                        lhs[:, tokens(c)], rhs[:, :, tokens(c)], start=True, stop=True)
            last.then_inc(done, 1)

        def cell_tensor(pe, cell, last=False):
            nxt = cell.shifted(1)
            e = e_t[:, cell.b % 2, :]
            pe.wait_ge(e_done, cell.count(1, 1))
            turned(pe, cell, "e", [e[:, tokens(c)] for c in range(CH)], e_turned)
            pe.wait_ge(k_done, cell.count(1, 1))
            turned(pe, cell, "k", [k_t[:, tokens(c)] for c in range(CH)], k_turned)
            pe.wait_ge(rz_done, cell.count(1, 1))
            turned(pe, cell, "rz", [rz_t[:, tokens(c)] for c in range(CH)], rz_turned)
            token_proj(pe, cell, 0)
            token_proj(pe, cell, 1)
            pe.wait_ge(q_done, cell.count(1, 1))
            if not first(cell):
                pe.wait_ge(y_done, cell.count(2 * CH, 0))
            pair_blocks(pe, 0, k_t, q_bd, scores)
            pair_blocks(pe, 1, k_t, q_bd, scores)
            if not first(cell):
                for half in range(2):
                    pe.wait_ge(y_done, cell.count(2 * CH, (half - 1) * CH))
                    turned(pe, cell, f"y{half}",
                           [y[:, c, h, :] for c in (2 * half, 2 * half + 1) for h in range(2)], y_turned)
            pe.wait_ge(e_tok_done, cell.count(1, 1))
            pe.wait_ge(k_tok_done, cell.count(1, 1))
            for c in range(CH):
                if c > 0:
                    pe.wait_ge(hk_kept, cell.count(CH - 1, c))
                if c < CH - 1:
                    nc.tensor.matmul(XB[:, 0:P], k_tok[:, c, :], e_tok[:, c, 1:3, :].rearrange("p h m -> p (h m)"),
                                     start=(c == 0), stop=True, skip_group_check=True).then_inc(hk_summed, 1)
                o = OB[:, c * P:(c + 1) * P]
                if c > 0:
                    nc.tensor.matmul(o, q_t[:, tokens(c)], hk[:, c - 1, :], start=True, stop=False)
                pe.wait_ge(scores_masked, cell.count(2, c // 2 + 1))
                nc.tensor.matmul(o.rearrange("p (h m) -> p h m", h=2), w_t[:, c, 0, :], e_tok[:, c, 1:4:2, :],
                                 start=(c == 0), stop=False)
                mm = nc.tensor.matmul(o.rearrange("p (h m) -> p h m", h=2), w_t[:, c, 1, :], e_tok[:, c, 0:3:2, :],
                                      start=False, stop=True)
            mm.then_inc(ok_summed, 1)
            if not first(cell):
                for c in range(CH):
                    output_rows(pe, cell, c)

            def running_values(c):
                pe.wait_ge(v_done, cell.count(CH, c + 1))
                if c > 0:
                    pe.wait_ge(hv_kept, cell.count(CH - 1, c))
                else:
                    pe.wait_ge(hk_kept, cell.count(CH - 1, CH - 1))
                nc.tensor.matmul(XB[:, P:P + VW], e_tok[:, c, 1:3, :].rearrange("p h m -> p (h m)"), v_tok[:, c, :], start=(c == 0),
                                 stop=True, skip_group_check=True).then_inc(hv_summed, 1)

            running_values(0)
            token_proj(pe, cell, 2)
            running_values(1)
            pe.wait_ge(pz_done, cell.count(1, 1))
            turned(pe, cell, "pz", [pz[:, c, :, :].rearrange("p h m -> p (h m)") for c in range(CH)], pz_turned)
            token_proj(pe, cell, 3)
            running_values(2)
            if not last:
                feature_proj(pe, nxt, 0, s_proj)
            pe.wait_ge(pz_t_done, cell.count(1, 1))
            pair_blocks(pe, 0, e, pz_bd, weights)
            pair_blocks(pe, 1, e, pz_bd, weights)
            if not last:
                feature_proj(pe, nxt, 1, q_proj)
                feature_proj(pe, nxt, 2, k_proj)
            pe.wait_ge(v_done, cell.count(CH, CH))
            for half in range(2):
                pe.wait_ge(weights_masked, cell.count(2, half + 1))
                for c in (2 * half, 2 * half + 1):
                    o = (OB, SB[0])[half][:, (c % 2) * VW:(c % 2 + 1) * VW]
                    if c > 0:
                        pe.wait_ge(hv_kept, cell.count(CH - 1, c))
                        nc.tensor.matmul(o, pz_t[:, tokens(c)], hv[:, c - 1, :], start=True, stop=False, skip_group_check=True)
                    for h in range(2):
                        mm = nc.tensor.matmul(o[:, h * DV:(h + 1) * DV], w_t[:, c, h, :],
                                              v_tok[:, c, h * DV:(h + 1) * DV],
                                              start=(c == 0), stop=True, skip_group_check=True)
                mm.then_inc(values, 1)

        @block.tensor
        def _(pe):
            pe.wait_ge(const_done, 5)
            for g in range(B * KT):
                b, kt = g // KT, g % KT
                if kt == 0:
                    pe.wait_ge(x_in[b], 16)
                if g >= 2:
                    pe.wait_ge(xt_lo_done, g - 1)
                for c in range(CH):
                    mm = nc.tensor.transpose(SB[g % 2][:, tokens(c)], acc[:, b * CH + c, kt * P:(kt + 1) * P], ident[:])
                mm.then_inc(xt_turned, 1)
            pe.wait_ge(xt_lo_done, B * KT)
            m = Cell(None, 0)
            feature_proj(pe, m, 0, s_proj)
            feature_proj(pe, m, 1, q_proj)
            feature_proj(pe, m, 2, k_proj)
            cell_tensor(pe, m)
            with pe.Fori(0, PAIRS - 1) as j:
                for b in range(1, B + 1):
                    cell_tensor(pe, Cell(j, b))
            for b in range(1, B):
                cell_tensor(pe, Cell(None, B * (PAIRS - 1) + b), last=b == B - 1)
            tail = Cell(None, CELLS)
            for half in range(2):
                pe.wait_ge(y_done, tail.count(2 * CH, (half - 1) * CH))
                turned(pe, tail, f"y{half}", [y[:, c, h, :] for c in (2 * half, 2 * half + 1) for h in range(2)], y_turned)
            for c in range(CH):
                output_rows(pe, tail, c)


def experts(nc, acc, ident, U, V, W1, b1, W2, b2, out):
    KR = K_EXP * R_EXP
    G = B
    ctx = ExitStack()
    with ctx:
        def sb(name, shape, dt=F32):
            return ctx.enter_context(nc.sbuf_tensor(name, shape, dt))

        def sem(name):
            return ctx.enter_context(nc.semaphore(name))

        w1_raw = sb("w1_raw", [P, KT, D])
        v_raw = sb("v_raw", [P, KT, D])
        u_raw = sb("u_raw", [P, KT, K_EXP, R_EXP])
        w1_hi, w1_lo = sb("w1_hi", [P, KT, D], F32R), sb("w1_lo", [P, KT, D], F32R)
        vt_hi, vt_lo = sb("vt_hi", [P, KT, KR], F32R), sb("vt_lo", [P, KT, KR], F32R)
        ut_hi, ut_lo = sb("ut_hi", [P, KT, D], F32R), sb("ut_lo", [P, KT, D], F32R)
        w2_pad = sb("w2_pad", [P, KT, P])
        b1_col = sb("b1_col", [P, KT])
        b2_row = sb("b2_row", [P, K_EXP])
        xs = sb("xs", [P, CH, D])
        x1t_hi, x1t_lo = sb("x1t_hi", [P, KT, T], F32R), sb("x1t_lo", [P, KT, T], F32R)
        ht = sb("ht", [P, KT, T])
        w = sb("w", [P, CH, K_EXP, R_EXP])
        wt_hi, wt_lo = sb("wt_hi", [P, CH, KT, P], F32R), sb("wt_lo", [P, CH, KT, P], F32R)
        alpha = sb("alpha", [P, CH, K_EXP])
        a_top, a_sum = sb("a_top", [P, CH]), sb("a_sum", [P, CH])
        st1, st2 = sb("st1", [P, CH, 6]), sb("st2", [P, CH, 6])
        mv1, mv2 = sb("mv1", [P, CH, 2]), sb("mv2", [P, CH, 2])
        va1, va2 = sb("va1", [P, CH]), sb("va2", [P, CH])
        rs1, rs2 = sb("rs1", [P, CH]), sb("rs2", [P, CH])
        half = sb("half", [P, CH])

        AB = [ctx.enter_context(nc.psum_tensor(f"a{i}", [P, BANK], F32)) for i in range(4)]
        LB = ctx.enter_context(nc.psum_tensor("l", [P, BANK], F32))
        XT = [ctx.enter_context(nc.psum_tensor(f"xt{i}", [P, BANK], F32)) for i in range(2)]
        WT = [ctx.enter_context(nc.psum_tensor("wt", [P, BANK], F32)), LB]

        w1_in, v_in, u_in, small_in, w2_in, out_sent = (
            sem("w1_in"), sem("v_in"), sem("u_in"), sem("small_in"), sem("w2_in"), sem("out_sent"))
        zeroed, half_set = sem("zeroed"), sem("half_set")
        prep_turned, prep_hi, prep_lo = sem("prep_turned"), sem("prep_hi"), sem("prep_lo")
        stats1, moments1, var1, rstd1, x1_done = sem("stats1"), sem("moments1"), sem("var1"), sem("rstd1"), sem("x1_done")
        stats2, moments2, var2, rstd2, x2_done = sem("stats2"), sem("moments2"), sem("var2"), sem("rstd2"), sem("x2_done")
        xs_done, x_turned, x_hi, x_lo = sem("xs_done"), sem("x_turned"), sem("x_hi"), sem("x_lo")
        h_proj, h_done, logits, vx = sem("h_proj"), sem("h_done"), sem("logits"), sem("vx")
        a_biased, a_topped, a_less_top, a_exp = sem("a_biased"), sem("a_topped"), sem("a_less_top"), sem("a_exp")
        a_summed, a_inverse, alpha_done = sem("a_summed"), sem("a_inverse"), sem("alpha_done")
        w_done, w_turned, w_hi, w_lo = sem("w_done"), sem("w_turned"), sem("w_hi"), sem("w_lo")
        rows, added = sem("f_rows"), sem("f_added")

        block = ctx.enter_context(nc.Block())

        def tile(g, t):
            if isinstance(g, int):
                return acc[:, g * CH + t, :]
            return acc[:, bass.ds(g * CH + t, 1), :].rearrange("p a d -> p (a d)")

        @block.sync
        def _(sp):
            sp.dma_start(v_raw[:], V.rearrange("k r d -> (k r) d").rearrange("(a p) d -> p a d", p=P)).then_inc(v_in, 16)
            sp.dma_start(w1_raw[:], W1.rearrange("(a p) n -> p a n", p=P)).then_inc(w1_in, 16)
            for kt in range(KT):
                sp.dma_start(u_raw[:, kt, :, :],
                             U.rearrange("k (a p) r -> a p k r", p=P)[kt]).then_inc(u_in, 16)
            for n in range(KT):
                sp.dma_start(b1_col[:, n:n + 1],
                             b1[n * P:(n + 1) * P].rearrange("(p a) -> p a", a=1)).then_inc(small_in, 16)
            sp.dma_start(b2_row[:], b2.partition_broadcast(P)).then_inc(small_in, 16)
            sp.wait_ge(zeroed, 1)
            sp.dma_start(w2_pad[:, :, 0:K_EXP], W2.rearrange("(a p) n -> p a n", p=P)).then_inc(w2_in, 16)
            ov = out.rearrange("b (t p) d -> p b t d", p=P)
            for g in range(G):
                for t in range(CH):
                    sp.wait_ge(x2_done, g * CH + t + 1)
                    sp.dma_start(ov[:, g, t, :], acc[:, g * CH + t, :]).then_inc(out_sent, 16)
            sp.wait_ge(out_sent, 16 * G * CH)

        @block.gpsimd
        def _(pool):
            nc.gpsimd.memset(half[:], -0.5).then_inc(half_set, 1)
            pool.wait_ge(half_set, 1)
            for g in range(G + 1):
                if g < G:
                    pool.wait_ge(var1, g + 1)
                    nc.gpsimd.tensor_tensor(rs1[:], va1[:], half[:], ALU.pow).then_inc(rstd1, 1)
                if g > 0:
                    pool.wait_ge(var2, g)
                    nc.gpsimd.tensor_tensor(rs2[:], va2[:], half[:], ALU.pow).then_inc(rstd2, 1)

        PE_TURNS = [("w", 0), ("w", 1), ("x", 0), ("x", 1), ("w", 2), ("x", 2), ("w", 3), ("x", 3)]

        def prep_part(n, which):
            m, k = divmod(n, KT)
            return ((vt_hi, vt_lo), (ut_hi, ut_lo), (w1_hi, w1_lo))[m][which][:, k, :]

        def prep_source(n):
            return AB[n % 4][:] if n < 2 * KT else w1_raw[:, n - 2 * KT, :]

        @block.scalar
        def _(act):
            def copy_x1(g):
                for t in range(CH):
                    act.wait_ge(x1_done, g * CH + t + 1)
                    nc.scalar.activation(xs[:, t, :], tile(g, t), ACT.Copy).then_inc(xs_done, 1)

            def x_high(g, kt):
                act.wait_ge(x_turned, g * KT + kt + 1)
                nc.scalar.activation(x1t_hi[:, kt, :], XT[kt % 2][:], ACT.Copy).then_inc(x_hi, 1)

            for n in range(3 * KT):
                if n < 2 * KT:
                    act.wait_ge(prep_turned, n + 1)
                elif n == 2 * KT:
                    act.wait_ge(w1_in, 16)
                nc.scalar.activation(prep_part(n, 0), prep_source(n), ACT.Copy).then_inc(prep_hi, 1)
            act.wait_ge(small_in, 16 * (KT + 1))
            copy_x1(0)
            for kt in range(KT):
                x_high(0, kt)

            def group(g, last):
                for n in range(KT):
                    act.wait_ge(h_proj, g * KT + n + 1)
                    nc.scalar.activation(ht[:, n, :], AB[n][:], ACT.Relu, bias=b1_col[:, n:n + 1]).then_inc(h_done, 1)
                act.wait_ge(a_less_top, g + 1)
                nc.scalar.activation(alpha[:], alpha[:], ACT.Exp).then_inc(a_exp, 1)
                if not last:
                    copy_x1(g + 1)
                for kind, k in PE_TURNS:
                    if kind == "w":
                        act.wait_ge(w_turned, g * CH + k + 1)
                        nc.scalar.activation(wt_hi[:, k, :, :].rearrange("p a t -> p (a t)"),
                                             WT[k % 2][:], ACT.Copy).then_inc(w_hi, 1)
                    elif not last:
                        x_high(g + 1, k)

            for g in range(G):
                group(g, g == G - 1)

        @block.vector
        def _(dve):
            def norm1(g):
                for t in range(CH):
                    nc.vector.bn_stats(out=st1[:, t, :], in_=tile(g, t)).then_inc(stats1, 1)
                    dve.wait_ge(stats1, g * CH + t + 1)
                    nc.vector.bn_aggr(out=mv1[:, t, :], in_=st1[:, t, :]).then_inc(moments1, 1)
                dve.wait_ge(moments1, (g + 1) * CH)
                nc.vector.tensor_scalar(va1[:], mv1[:, :, 1], EPS, None, ALU.add).then_inc(var1, 1)
                dve.wait_ge(rstd1, g + 1)
                for t in range(CH):
                    nc.vector.tensor_scalar(tile(g, t), tile(g, t), mv1[:, t, 0:1], rs1[:, t:t + 1],
                                            ALU.subtract, ALU.mult).then_inc(x1_done, 1)

            def x_low(g, kt):
                dve.wait_ge(x_hi, g * KT + kt + 1)
                nc.vector.tensor_tensor(x1t_lo[:, kt, :], XT[kt % 2][:],
                                        x1t_hi[:, kt, :].bitcast(F32), ALU.subtract).then_inc(x_lo, 1)

            nc.vector.memset(w2_pad[:], 0.0).then_inc(zeroed, 1)
            norm1(0)
            for n in range(3 * KT):
                dve.wait_ge(prep_hi, n + 1)
                nc.vector.tensor_tensor(prep_part(n, 1), prep_source(n), prep_part(n, 0).bitcast(F32),
                                        ALU.subtract).then_inc(prep_lo, 1)
            for kt in range(KT):
                x_low(0, kt)

            def add_tile(g, t):
                dve.wait_ge(rows, g * CH + t + 1)
                nc.vector.tensor_tensor(tile(g, t), AB[t][:], tile(g, t), ALU.add).then_inc(added, 1)
                dve.wait_ge(added, g * CH + t + 1)
                nc.vector.bn_stats(out=st2[:, t, :], in_=tile(g, t)).then_inc(stats2, 1)
                dve.wait_ge(stats2, g * CH + t + 1)
                nc.vector.bn_aggr(out=mv2[:, t, :], in_=st2[:, t, :]).then_inc(moments2, 1)

            def norm2(g):
                dve.wait_ge(rstd2, g + 1)
                for t in range(CH):
                    nc.vector.tensor_scalar(tile(g, t), tile(g, t), mv2[:, t, 0:1], rs2[:, t:t + 1],
                                            ALU.subtract, ALU.mult).then_inc(x2_done, 1)

            def group(g, last):
                if not last:
                    norm1(g + 1)
                if g > 0:
                    norm2(g - 1)
                dve.wait_ge(logits, g + 1)
                nc.vector.tensor_tensor(alpha[:], LB[:].rearrange("p (t n) -> p t n", t=CH)[:, :, 0:K_EXP],
                                        b2_row[:].rearrange("p (a k) -> p a k", a=1).broadcast_to([P, CH, K_EXP]),
                                        ALU.add).then_inc(a_biased, 1)
                dve.wait_ge(a_biased, g + 1)
                nc.vector.tensor_reduce(a_top[:], alpha[:], AX_X, ALU.max).then_inc(a_topped, 1)
                dve.wait_ge(a_topped, g + 1)
                nc.vector.tensor_tensor(alpha[:], alpha[:],
                                        a_top[:].rearrange("p (t a) -> p t a", a=1).broadcast_to([P, CH, K_EXP]),
                                        ALU.subtract).then_inc(a_less_top, 1)
                dve.wait_ge(a_exp, g + 1)
                nc.vector.tensor_reduce(a_sum[:], alpha[:], AX_X, ALU.add).then_inc(a_summed, 1)
                dve.wait_ge(a_summed, g + 1)
                nc.vector.reciprocal(a_sum[:], a_sum[:]).then_inc(a_inverse, 1)
                dve.wait_ge(a_inverse, g + 1)
                nc.vector.tensor_tensor(alpha[:], alpha[:],
                                        a_sum[:].rearrange("p (t a) -> p t a", a=1).broadcast_to([P, CH, K_EXP]),
                                        ALU.mult).then_inc(alpha_done, 1)
                dve.wait_ge(alpha_done, g + 1)
                for t in range(CH):
                    dve.wait_ge(vx, g * CH + t + 1)
                    nc.vector.tensor_tensor(
                        w[:, t, :, :], AB[t][:].rearrange("p (k r) -> p k r", k=K_EXP),
                        alpha[:, t, :].rearrange("p (k a) -> p k a", a=1).broadcast_to([P, K_EXP, R_EXP]),
                        ALU.mult).then_inc(w_done, 1)
                adds = 0
                for kind, k in PE_TURNS:
                    if kind == "w":
                        dve.wait_ge(w_hi, g * CH + k + 1)
                        nc.vector.tensor_tensor(wt_lo[:, k, :, :].rearrange("p a t -> p (a t)"), WT[k % 2][:],
                                                wt_hi[:, k, :, :].rearrange("p a t -> p (a t)").bitcast(F32),
                                                ALU.subtract).then_inc(w_lo, 1)
                    elif not last:
                        x_low(g + 1, k)
                for t in range(CH):
                    add_tile(g, t)
                dve.wait_ge(moments2, (g + 1) * CH)
                nc.vector.tensor_scalar(va2[:], mv2[:, :, 1], EPS, None, ALU.add).then_inc(var2, 1)

            for g in range(G):
                group(g, g == G - 1)
            norm2(G - 1)

        @block.tensor
        def _(pe):
            def split_product(out_, terms, done):
                n = len(terms)
                for k, ((lh, ll), (rh, rl)) in enumerate(terms):
                    nc.tensor.matmul(out_, lh, rh, start=(k == 0), stop=False)
                    nc.tensor.matmul(out_, lh, rl, start=False, stop=False)
                    last = nc.tensor.matmul(out_, ll, rh, start=False, stop=(k == n - 1))
                last.then_inc(done, 1)

            def tokens(t):
                return slice(t * P, (t + 1) * P)

            def blocks(bank_, blks, done):
                for i, blk in enumerate(blks):
                    mm = nc.tensor.transpose(bank_[:, tokens(i)], blk, ident[:])
                mm.then_inc(done, 1)

            for n in range(2 * KT):
                m, k = divmod(n, KT)
                if k == 0:
                    pe.wait_ge((v_in, u_in)[m], (16, 16 * KT)[m])
                if n >= 4:
                    pe.wait_ge(prep_lo, n - 3)
                if m == 0:
                    blks = [v_raw[:, i, k * P:(k + 1) * P] for i in range(KT)]
                else:
                    blks = [u_raw[:, i, 2 * k:2 * k + 2, :].rearrange("p k r -> p (k r)") for i in range(KT)]
                blocks(AB[n % 4], blks, prep_turned)

            def x_turn(g, kt):
                if g * KT + kt >= 2:
                    pe.wait_ge(x_lo, g * KT + kt - 1)
                pe.wait_ge(xs_done, (g + 1) * CH)
                blocks(XT[kt % 2], [xs[:, t, kt * P:(kt + 1) * P] for t in range(CH)], x_turned)

            for kt in range(KT):
                x_turn(0, kt)
            pe.wait_ge(prep_lo, 3 * KT)
            pe.wait_ge(w2_in, 16)

            def group(g, last):
                pe.wait_ge(x_lo, (g + 1) * KT)
                for n in range(KT):
                    if g > 0:
                        pe.wait_ge(added, (g - 1) * CH + n + 1)
                    split_product(AB[n][:], [((w1_hi[:, kt, tokens(n)], w1_lo[:, kt, tokens(n)]),
                                              (x1t_hi[:, kt, :], x1t_lo[:, kt, :])) for kt in range(KT)], h_proj)

                def vx_tile(t):
                    pe.wait_ge(h_done, g * KT + t + 1)
                    split_product(AB[t][:], [((x1t_hi[:, kt, tokens(t)], x1t_lo[:, kt, tokens(t)]),
                                              (vt_hi[:, kt, :], vt_lo[:, kt, :])) for kt in range(KT)], vx)

                vx_tile(0)
                pe.wait_ge(h_done, (g + 1) * KT)
                for t in range(CH):
                    for n in range(KT):
                        mm = nc.tensor.matmul(LB[:, tokens(t)], ht[:, n, tokens(t)], w2_pad[:, n, :],
                                              start=(n == 0), stop=(n == KT - 1))
                mm.then_inc(logits, 1)
                for t in range(1, CH):
                    vx_tile(t)

                def turn_one(i):
                    kind, k = PE_TURNS[i]
                    if kind == "w":
                        pe.wait_ge(w_done, g * CH + k + 1)
                        if g * CH + k >= 2:
                            pe.wait_ge(w_lo, g * CH + k - 1)
                        blocks(WT[k % 2], [w[:, k, 2 * n:2 * n + 2, :].rearrange("p k r -> p (k r)") for n in range(KT)],
                               w_turned)
                    elif not last:
                        x_turn(g + 1, k)

                def out_tile(t):
                    pe.wait_ge(w_lo, g * CH + t + 1)
                    split_product(AB[t][:], [((wt_hi[:, t, n, :], wt_lo[:, t, n, :]),
                                              (ut_hi[:, n, :], ut_lo[:, n, :])) for n in range(KT)], rows)

                for i in range(4):
                    turn_one(i)
                out_tile(0)
                turn_one(4)
                turn_one(5)
                out_tile(1)
                turn_one(6)
                turn_one(7)
                out_tile(2)
                out_tile(3)

            for g in range(G):
                group(g, g == G - 1)


_INS = ["L0_attn_hidden_states", "L0_attn_Wq", "L0_attn_Wk", "L0_attn_Wv", "L0_attn_Wg", "L0_attn_Ws", "L0_attn_Wo",
        "L0_attn_g_norm_weight", "L0_ffn_U", "L0_ffn_V", "L0_ffn_W1", "L0_ffn_b1", "L0_ffn_W2", "L0_ffn_b2"]
_OUT = (B, T, D)


def kernel(**inputs):
    import numpy as _np
    import concourse.bacc as _bacc
    from concourse import mybir as _mybir
    from concourse.bass_utils import run_bass_kernel_spmd as _run

    nc = _bacc.Bacc("TRN2", target_bir_lowering=False, num_devices=1)
    arrays, args = {}, []
    for name in _INS:
        a = _np.ascontiguousarray(inputs[name])
        arrays[f"in_{name}"] = a
        args.append(nc.dram_tensor(f"in_{name}", a.shape, _mybir.dt.from_np(a.dtype), kind="ExternalInput").ap())
    args.append(nc.dram_tensor("out", _OUT, _mybir.dt.float32, kind="ExternalOutput").ap())
    build(nc, *args)
    r = _run(nc, [arrays], core_ids=[0])
    return r.results[0]["out"]
```

```python
from contextlib import ExitStack

import concourse.bass as bass
from concourse import mybir
from concourse.alu_op_type import AluOpType as ALU

ACT = mybir.ActivationFunctionType
F32 = mybir.dt.float32
F32R = mybir.dt.float32r
AX_X = mybir.AxisListType.X

P = 128
BANK = 512

B, T, D = 4, 512, 512
H, DK, DV, M = 16, 64, 128, 64
R_KEEP, K_EXP, R_EXP = 128, 8, 64
CLAMP = 32.0
EPS = 1e-5

KT = D // P
PAIRS = H // 2
CH = T // P
CELLS = PAIRS * B
VW = 2 * DV
NT = B * CH


class Cell:

    def __init__(self, j, b):
        self.j, self.b = j, b

    def shifted(self, by):
        return Cell(self.j, self.b + by)

    @property
    def batch(self):
        return self.b % B

    def count(self, per_cell, k=0):
        fixed = per_cell * self.b + k
        return fixed if self.j is None else self.j * (per_cell * B) + fixed


P_USES = ["vg0", "vg1", "wo0", "wo1", "wo2", "wo3", "vg2", "vg3", "s", "q", "k"]
T_USES = ["e", "k", "rz", "y0", "y1", "pz"]


def turn(cell, use, uses, start):
    def order(number):
        if number == 0:
            return [u for u in uses if u[:2] != "wo" and u[0] != "y"]
        if number == CELLS:
            return [u for u in uses if u[:2] == "wo" or u[0] == "y"]
        if number == CELLS - 1 and uses is P_USES:
            return [u for u in uses if u not in ("s", "q", "k")]
        return uses

    line = [(-1, u) for u in start]
    line += [(n, u) for n in range(cell.b + 1) for u in order(n)]
    at = line.index((cell.b, use))
    n, before = line[at - 2] if at >= 2 else (None, None)
    return at % 2, None if n is None else (cell.shifted(n - cell.b), before)


def p_turn(cell, use):
    return turn(cell, use, P_USES, ["s", "q", "k"])


def t_turn(cell, use):
    return turn(cell, use, T_USES, [])


def build(nc, x, Wq, Wk, Wv, Wg, Ws, Wo, g_norm, U, V, W1, b1, W2, b2, out):
    with ExitStack() as whole:
        acc = whole.enter_context(nc.sbuf_tensor("acc", [P, NT, D], F32))
        ident = whole.enter_context(nc.sbuf_tensor("ident", [P, P], F32))
        v_in, w1_in, u_in = [whole.enter_context(nc.semaphore(n)) for n in ("v_in", "w1_in", "u_in")]
        raws = attention(nc, acc, ident, (U, V, W1), (u_in, v_in, w1_in), x, Wq, Wk, Wv, Wg, Ws, Wo, g_norm)
        experts(nc, acc, ident, raws, (u_in, v_in, w1_in), b1, W2, b2, out)


def attention(nc, acc, ident, expert_weights, expert_sems, x, Wq, Wk, Wv, Wg, Ws, Wo, g_norm):
    ctx = ExitStack()
    with ctx:
        def sb(name, shape, dt=F32):
            return ctx.enter_context(nc.sbuf_tensor(name, shape, dt))

        def bank(name):
            return ctx.enter_context(nc.psum_tensor(name, [P, BANK], F32))

        def sem(name):
            return ctx.enter_context(nc.semaphore(name))

        with ExitStack() as early:
            v_raw = early.enter_context(nc.sbuf_tensor("v_raw", [P, KT, D], F32))
            u_raw = early.enter_context(nc.sbuf_tensor("u_raw", [P, KT, K_EXP, R_EXP], F32))
            w1_raw = early.enter_context(nc.sbuf_tensor("w1_raw", [P, KT, D], F32))
        xt_hi, xt_lo = [], []
        for b in range(B):
            xt_hi.append(sb(f"xt_hi{b}", [P, KT, T], F32R))
            xt_lo.append(sb(f"xt_lo{b}", [P, KT, T], F32R))
        wsqk_hi = sb("wsqk_hi", [P, 3, KT, P], F32R)
        wsqk_lo = sb("wsqk_lo", [P, 3, KT, P], F32R)
        wvg_hi = sb("wvg_hi", [P, KT, 2 * VW], F32R)
        wvg_lo = sb("wvg_lo", [P, KT, 2 * VW], F32R)
        wo_hi = sb("wo_hi", [P, 2, D], F32R)
        wo_lo = sb("wo_lo", [P, 2, D], F32R)
        raw = sb("raw", [P, 3, BANK])
        e_t = sb("e_t", [P, 2, T])
        rz_t = sb("rz_t", [P, T])
        q_t = sb("q_t", [P, T])
        bd_hi, bd_lo = sb("bd_hi", [P, 2, T], F32R), sb("bd_lo", [P, 2, T], F32R)
        lhs_hi, lhs_lo = sb("lhs_hi", [P, T], F32R), sb("lhs_lo", [P, T], F32R)
        k_t = sb("k_t", [P, T])
        e_tok = sb("e_tok", [P, CH, 4, M])
        k_tok = sb("k_tok", [P, CH, P])
        rz_tok = sb("rz_tok", [P, CH, P])
        w_t = sb("w_t", [P, CH, 2, P])
        hk = sb("hk", [P, CH - 1, P])
        hv = sb("hv", [P, CH - 1, VW])
        ok = sb("ok", [P, CH, 2, M])
        pz = sb("pz", [P, CH, 2, M])
        pz_t = sb("pz_t", [P, T])
        v_tok = sb("v_tok", [P, CH, VW])
        gate = sb("gate", [P, CH, VW])
        th = sb("th", [P, 2, VW])
        y = sb("y", [P, CH, 2, DV])
        yt_hi = sb("yt_hi", [P, 2, 2, 2, P], F32R)
        yt_lo = sb("yt_lo", [P, 2, 2, 2, P], F32R)
        causal = sb("causal", [P, P])
        own = sb("own", [P, 2, DV])
        gn = sb("gn", [P, 2])
        top = sb("top", [P, 2 * CH])
        esum = sb("esum", [P, 2 * CH])
        esq = sb("esq", [P, 2 * CH])
        osq = sb("osq", [P, 2 * CH])
        ovar = sb("ovar", [P, 2 * CH])
        orstd = sb("orstd", [P, 2 * CH])
        minus_half = sb("minus_half", [P, 2 * CH])

        PB = [bank("p0"), bank("p1")]
        TB = [bank("t0"), bank("t1")]
        SB = [bank("s0"), bank("s1")]
        OB = bank("o")
        XB = bank("xb")
        XTB = [SB[0], SB[1], OB, XB]

        x_in = [sem(f"x_in{b}") for b in range(B)]
        raw_in = [sem(f"raw_in{i}") for i in range(3)]
        gn_in = sem("gn_in")
        w_hi_done = sem("w_hi_done")
        w_lo_done = sem("w_lo_done")
        wo_hi_done = sem("wo_hi_done")
        wo_lo_done = sem("wo_lo_done")
        const_done = sem("const_done")
        own_done = sem("own_done")
        gn_half = sem("gn_half")
        xt_turned = sem("xt_turned")
        xt_hi_done = sem("xt_hi_done")
        xt_lo_done = sem("xt_lo_done")
        s_proj, q_proj, k_proj, vg_proj = sem("s_proj"), sem("q_proj"), sem("k_proj"), sem("vg_proj")
        e_turned, k_turned, rz_turned = sem("e_turned"), sem("k_turned"), sem("rz_turned")
        y_turned, pz_turned = sem("y_turned"), sem("pz_turned")
        scores = sem("scores")
        hk_summed, ok_summed, hv_summed = sem("hk_summed"), sem("ok_summed"), sem("hv_summed")
        weights, values, rows = sem("weights"), sem("values"), sem("rows")
        s_clipped, e_done, z_done, rz_done = sem("s_clipped"), sem("e_done"), sem("z_done"), sem("rz_done")
        q_done, k_done, v_done, th_done, gate_done = (
            sem("q_done"), sem("k_done"), sem("v_done"), sem("th_done"), sem("gate_done"))
        e_tok_done, k_tok_done, rz_tok_done = sem("e_tok_done"), sem("k_tok_done"), sem("rz_tok_done")
        scores_masked, weights_masked = sem("scores_masked"), sem("weights_masked")
        hk_kept, hv_kept = sem("hk_kept"), sem("hv_kept")
        ok_scaled, top_done, ok_less_top, exp_done = (
            sem("ok_scaled"), sem("top_done"), sem("ok_less_top"), sem("exp_done"))
        pz_done, esum_done, esq_done = sem("pz_done"), sem("esum_done"), sem("esq_done")
        pz_t_done, pz_lo_done = sem("pz_t_done"), sem("pz_lo_done")
        q_lo_done, k_lo_done = sem("q_lo_done"), sem("k_lo_done")
        e_hi_done, e_lo_done = sem("e_hi_done"), sem("e_lo_done")
        osq_done, ovar_done, orstd_done = sem("osq_done"), sem("ovar_done"), sem("orstd_done")
        y_done, yt_hi_done, yt_lo_done = sem("y_done"), sem("yt_hi_done"), sem("yt_lo_done")
        added = sem("added")

        def tokens(c):
            return slice(c * P, (c + 1) * P)

        def load_piece(sp, J, name, i):
            slot = raw[:, i % 3, :]
            if name == "sqk":
                w = (Ws, Wq, Wk)[i]
                src = w.rearrange("(k p) n -> p k n", p=P)[:, :, bass.ds(J * P, P)]
                sp.dma_start(slot.rearrange("p (k n) -> p k n", k=KT), src).then_inc(raw_in[i % 3], 16)
            elif name == "vg":
                kt = i - 3
                for half, w in ((0, Wv), (1, Wg)):
                    src = w[kt * P:(kt + 1) * P, bass.ds(J * VW, VW)]
                    sp.dma_start(slot[:, half * VW:(half + 1) * VW], src).then_inc(raw_in[i % 3], 16)
            else:
                h = i - 7
                src = Wo[bass.ds(J * VW + h * DV, DV), :]
                sp.dma_start(slot, src).then_inc(raw_in[i % 3], 16)

        LANDED = {0: (0, 1), 3: (0, 3), 6: (0, 5), 1: (1, 1), 4: (1, 3), 7: (1, 4), 2: (2, 1), 5: (2, 3), 8: (2, 4)}
        PER_PAIR = (5, 4, 4)

        def wait_landed(eng, J, i):
            slot, k = LANDED[i]
            eng.wait_ge(raw_in[slot], J * (16 * PER_PAIR[slot]) + 16 * k)

        def name_of(i):
            return "sqk" if i < 3 else "vg" if i < 7 else "wo"

        def part(i, which):
            if i < 3:
                return (wsqk_hi, wsqk_lo)[which][:, i, :, :].rearrange("p k n -> p (k n)")
            if i < 7:
                return (wvg_hi, wvg_lo)[which][:, i - 3, :]
            return (wo_hi, wo_lo)[which][:, i - 7, :]

        def first(cell):
            return cell.j is None and cell.b == 0

        block = ctx.enter_context(nc.Block())

        @block.sync
        def _(sp):
            sp.dma_start(gn[:, 0:1], g_norm.rearrange("(p a) -> p a", a=1)).then_inc(gn_in, 16)
            xv = x.rearrange("b (n p) d -> b p n d", p=P)
            sp.dma_start(acc[:, 0:CH, :], xv[0]).then_inc(x_in[0], 16)
            for i in range(3):
                load_piece(sp, 0, name_of(i), i)
            for b in range(1, B - 1):
                sp.dma_start(acc[:, b * CH:(b + 1) * CH, :], xv[b]).then_inc(x_in[b], 16)
            for i in range(3, 9):
                sp.wait_ge(w_lo_done, i - 2)
                load_piece(sp, 0, name_of(i), i)
                if i == 5:
                    sp.dma_start(acc[:, (B - 1) * CH:B * CH, :], xv[B - 1]).then_inc(x_in[B - 1], 16)
            with sp.Fori(1, PAIRS) as J:
                for i in range(9):
                    if i == 0:
                        sp.wait_ge(w_lo_done, J * 7)
                    elif i < 3:
                        sp.wait_ge(wo_lo_done, J * 2 + (i - 2))
                    else:
                        sp.wait_ge(w_lo_done, J * 7 + (i - 2))
                    load_piece(sp, J, name_of(i), i)
            U, V, W1 = expert_weights
            u_in, v_in, w1_in = expert_sems
            sp.wait_ge(vg_proj, CH * (CELLS - B + 1))
            sp.dma_start(v_raw[:], V.rearrange("k r d -> (k r) d").rearrange("(a p) d -> p a d", p=P)).then_inc(v_in, 16)
            for kt in range(KT):
                sp.dma_start(u_raw[:, kt, :, :],
                             U.rearrange("k (a p) r -> a p k r", p=P)[kt]).then_inc(u_in, 16)
            sp.wait_ge(vg_proj, CH * (CELLS - B + 2))
            sp.dma_start(w1_raw[:], W1.rearrange("(a p) n -> p a n", p=P)).then_inc(w1_in, 16)

        def split_low(pool, J, i):
            pool.wait_ge(w_hi_done, J * 7 + (i + 1))
            nc.gpsimd.tensor_tensor(part(i, 1), raw[:, i % 3, :], part(i, 0).bitcast(F32),
                                    ALU.subtract).then_inc(w_lo_done, 1)

        def keys_low(pool, m):
            pool.wait_ge(k_done, m.count(1, 1))
            nc.gpsimd.tensor_tensor(lhs_lo[:], k_t[:], lhs_hi[:].bitcast(F32), ALU.subtract).then_inc(k_lo_done, 1)

        def cell_gpsimd(pool, cell, J=None, last=False):
            if J is not None:
                for i in range(3):
                    split_low(pool, J, i)
            pool.wait_ge(e_hi_done, cell.count(1, 1))
            nc.gpsimd.tensor_tensor(lhs_lo[:], e_t[:, cell.b % 2, :], lhs_hi[:].bitcast(F32),
                                    ALU.subtract).then_inc(e_lo_done, 1)
            if J is not None:
                for i in range(3, 7):
                    split_low(pool, J, i)
            if not last:
                keys_low(pool, cell.shifted(1))
            pool.wait_ge(ovar_done, cell.count(1, 1))
            nc.gpsimd.tensor_tensor(orstd[:], ovar[:], minus_half[:], ALU.pow).then_inc(orstd_done, 1)

        @block.gpsimd
        def _(pool):
            pool.wait_ge(own_done, 2)
            nc.gpsimd.affine_select(out=ident[:], in_=ident[:], compare_op=ALU.not_equal, fill=1.0, base=0,
                                    pattern=[[-1, P]], channel_multiplier=1).then_inc(const_done, 1)
            nc.gpsimd.affine_select(out=causal[:], in_=causal[:], compare_op=ALU.is_ge, fill=0.0, base=0,
                                    pattern=[[1, P]], channel_multiplier=-1).then_inc(const_done, 1)
            nc.gpsimd.memset(minus_half[:], -0.5).then_inc(const_done, 1)
            for i in range(7):
                split_low(pool, 0, i)
            pool.wait_ge(const_done, 3)
            keys_low(pool, Cell(None, 0))
            cell_gpsimd(pool, Cell(None, 0))
            with pool.Fori(0, PAIRS - 1) as j:
                for b in range(1, B + 1):
                    cell_gpsimd(pool, Cell(j, b), j + 1 if b == 3 else None)
            for b in range(1, B):
                cell_gpsimd(pool, Cell(None, B * (PAIRS - 1) + b), last=b == B - 1)

        def split_high(act, J, i, release):
            wait_landed(act, J, i)
            if release is not None:
                act.wait_ge(*release)
            if i < 7:
                nc.scalar.activation(part(i, 0), raw[:, i % 3, :], ACT.Copy).then_inc(w_hi_done, 1)
            else:
                nc.scalar.activation(part(i, 0), raw[:, i % 3, :], ACT.Copy,
                                     scale=gn[:, 1:2]).then_inc(wo_hi_done, 1)

        def slots_scalar(act, m):
            act.wait_ge(s_clipped, m.count(1, 1))
            e = e_t[:, m.b % 2, :]
            nc.scalar.activation(e, e, ACT.Exp).then_inc(e_done, 1)

        def queries_scalar(act, m):
            bk, _ = p_turn(m.shifted(-1), "q")
            ps = PB[bk]
            act.wait_ge(q_proj, m.count(1, 1))
            scale = float(DK) ** -0.5
            nc.scalar.activation(q_t[:], ps[:], ACT.Copy, scale=scale)
            nc.scalar.activation(bd_hi[0:DK, 0, :], ps[0:DK, :], ACT.Copy, scale=scale)
            nc.scalar.activation(bd_hi[DK:P, 1, :], ps[DK:P, :], ACT.Copy, scale=scale).then_inc(q_done, 1)

        def keys_scalar(act, m):
            bk, _ = p_turn(m.shifted(-1), "k")
            act.wait_ge(k_proj, m.count(1, 1))
            nc.scalar.activation(k_t[:], PB[bk][:], ACT.Copy)
            nc.scalar.activation(lhs_hi[:], PB[bk][:], ACT.Copy).then_inc(k_done, 1)

        def values_scalar(act, cell, c):
            bk, _ = p_turn(cell, f"vg{c}")
            act.wait_ge(vg_proj, cell.count(CH, c + 1))
            nc.scalar.activation(v_tok[:, c, :], PB[bk][:, 0:VW], ACT.Copy).then_inc(v_done, 1)
            if c >= 2 or not first(cell):
                act.wait_ge(gate_done, cell.count(CH, c - 1))
            nc.scalar.activation(th[:, c % 2, :], PB[bk][:, VW:2 * VW], ACT.Tanh,
                                 scale=0.5).then_inc(th_done, 1)

        def y_high(act, cell, half):
            prev = cell.shifted(-1)
            bk, _ = t_turn(cell, f"y{half}")
            act.wait_ge(y_turned, prev.count(2, half + 1))
            nc.scalar.activation(yt_hi[:, half, :, :, :].rearrange("p c h t -> p (c h t)"), TB[bk][:],
                                 ACT.Copy).then_inc(yt_hi_done, 1)

        def cell_scalar(act, cell, J=None, wo_J=None, last=False):
            nxt = cell.shifted(1)
            bk, _ = t_turn(cell, "e")
            act.wait_ge(e_turned, cell.count(1, 1))
            nc.scalar.activation(e_tok[:, :, 1:3, :], TB[bk][:].rearrange("p (c h m) -> p c h m", c=CH, h=2),
                                 ACT.Copy).then_inc(e_tok_done, 1)
            bk, _ = t_turn(cell, "k")
            act.wait_ge(k_turned, cell.count(1, 1))
            nc.scalar.activation(k_tok[:].rearrange("p c n -> p (c n)"), TB[bk][:], ACT.Copy).then_inc(k_tok_done, 1)
            if J is not None:
                for i, used in ((0, s_proj), (1, q_proj), (2, k_proj)):
                    split_high(act, J, i, (used, J * B))
            values_scalar(act, cell, 0)
            values_scalar(act, cell, 1)
            bk, _ = t_turn(cell, "rz")
            act.wait_ge(rz_turned, cell.count(1, 1))
            nc.scalar.activation(rz_tok[:].rearrange("p c n -> p (c n)"), TB[bk][:], ACT.Copy).then_inc(rz_tok_done, 1)
            act.wait_ge(scores, cell.count(2, 2))
            nc.scalar.activation(lhs_hi[:], e_t[:, cell.b % 2, :], ACT.Copy).then_inc(e_hi_done, 1)
            if not first(cell):
                y_high(act, cell, 0)
                y_high(act, cell, 1)
            act.wait_ge(ok_less_top, cell.count(1, 1))
            flat = ok[:].rearrange("p c h m -> p (c h m)")
            nc.scalar.activation(flat, flat, ACT.Exp).then_inc(exp_done, 1)
            values_scalar(act, cell, 2)
            bk, _ = t_turn(cell, "pz")
            act.wait_ge(pz_turned, cell.count(1, 1))
            nc.scalar.activation(pz_t[:], TB[bk][:], ACT.Copy)
            nc.scalar.activation(bd_hi[0:M, 0, :], TB[bk][0:M, :], ACT.Copy)
            nc.scalar.activation(bd_hi[M:P, 1, :], TB[bk][M:P, :], ACT.Copy).then_inc(pz_t_done, 1)
            values_scalar(act, cell, 3)
            if J is not None:
                for i in range(3, 7):
                    split_high(act, J, i, (vg_proj, J * (B * CH)))
            if not last:
                slots_scalar(act, nxt)
                queries_scalar(act, nxt)
                keys_scalar(act, nxt)
            if wo_J is not None:
                for i in (7, 8):
                    split_high(act, wo_J, i, (rows, wo_J * (B * CH)))
            for half in range(2):
                ps = (OB, SB[0])[half]
                act.wait_ge(values, cell.count(2, half + 1))
                for c in range(2):
                    for h in range(2):
                        g = (2 * half + c) * 2 + h
                        nc.scalar.activation(y[:, 2 * half + c, h, :], ps[:, (2 * c + h) * DV:(2 * c + h + 1) * DV],
                                             ACT.Square, accum_out=osq[:, g:g + 1]).then_inc(osq_done, 1)

        @block.scalar
        def _(act):
            act.wait_ge(gn_in, 16)
            nc.scalar.activation(gn[:, 1:2], gn[:, 0:1], ACT.Copy, scale=0.5).then_inc(gn_half, 1)

            def x_high(b):
                for kt in range(KT):
                    g = b * KT + kt
                    act.wait_ge(xt_turned, g + 1)
                    nc.scalar.activation(xt_hi[b][:, kt, :], XTB[g % 4][:], ACT.Copy).then_inc(xt_hi_done, 1)

            split_high(act, 0, 0, None)
            x_high(0)
            split_high(act, 0, 1, None)
            split_high(act, 0, 2, None)
            slots_scalar(act, Cell(None, 0))
            split_high(act, 0, 3, None)
            x_high(1)
            split_high(act, 0, 4, None)
            queries_scalar(act, Cell(None, 0))
            split_high(act, 0, 5, None)
            split_high(act, 0, 6, None)
            x_high(2)
            keys_scalar(act, Cell(None, 0))
            x_high(3)
            act.wait_ge(gn_half, 1)
            for i in (7, 8):
                split_high(act, 0, i, None)
            cell_scalar(act, Cell(None, 0))
            with act.Fori(0, PAIRS - 1) as j:
                for b in range(1, B + 1):
                    cell_scalar(act, Cell(j, b), j + 1 if b == 3 else None, j + 1 if b == 4 else None)
            for b in range(1, B):
                cell_scalar(act, Cell(None, B * (PAIRS - 1) + b), last=b == B - 1)
            y_high(act, Cell(None, CELLS), 0)
            y_high(act, Cell(None, CELLS), 1)

        def slots_vector(dve, m):
            bk, _ = p_turn(m.shifted(-1), "s")
            dve.wait_ge(s_proj, m.count(1, 1))
            nc.vector.tensor_scalar(e_t[:, m.b % 2, :], PB[bk][:], -CLAMP, CLAMP, ALU.max,
                                    ALU.min).then_inc(s_clipped, 1)

        def sums_vector(dve, m):
            dve.wait_ge(e_done, m.count(1, 1))
            e = e_t[:, m.b % 2, :]
            nc.vector.tensor_tensor_scan(rz_t[:], e, e, 0.0, ALU.add, ALU.bypass).then_inc(z_done, 1)

        def inverse_vector(dve, m):
            dve.wait_ge(z_done, m.count(1, 1))
            nc.vector.reciprocal(rz_t[:], rz_t[:]).then_inc(rz_done, 1)

        def queries_low(dve, m):
            bk, _ = p_turn(m.shifted(-1), "q")
            dve.wait_ge(q_done, m.count(1, 1))
            for h, own_rows in enumerate((slice(0, DK), slice(DK, P))):
                low = nc.vector.scalar_tensor_tensor(out=bd_lo[own_rows, h, :], in0=PB[bk][own_rows, :],
                                                     scalar=float(DK) ** -0.5,
                                                     in1=bd_hi[own_rows, h, :].bitcast(F32), op0=ALU.mult,
                                                     op1=ALU.subtract)
            low.then_inc(q_lo_done, 1)

        def masked(dve, cell, half, ready, done):
            dve.wait_ge(ready, cell.count(2, half + 1))
            nc.vector.tensor_tensor(
                w_t[:, 2 * half:2 * half + 2, :, :].rearrange("p c h t -> p (c h) t"),
                SB[half][:].rearrange("p (a t) -> p a t", a=4),
                causal[:].rearrange("p (a t) -> p a t", a=1).broadcast_to([P, 4, P]),
                ALU.mult).then_inc(done, 1)

        def gate_vector(dve, cell, c):
            bk, _ = p_turn(cell, f"vg{c}")
            dve.wait_ge(th_done, cell.count(CH, c + 1))
            if c == 0 and not first(cell):
                dve.wait_ge(y_done, cell.count(2 * CH, 0))
            nc.vector.scalar_tensor_tensor(out=gate[:, c, :], in0=th[:, c % 2, :], scalar=1.0,
                                           in1=PB[bk][:, VW:2 * VW], op0=ALU.add,
                                           op1=ALU.mult).then_inc(gate_done, 1)

        def y_vector(dve, prev):
            dve.wait_ge(orstd_done, prev.count(1, 1))
            dve.wait_ge(gate_done, prev.count(CH, CH))
            for half in range(2):
                ps = (OB, SB[0])[half]
                for c in range(2):
                    for h in range(2):
                        g = (2 * half + c) * 2 + h
                        nc.vector.scalar_tensor_tensor(
                            out=y[:, 2 * half + c, h, :], in0=ps[:, (2 * c + h) * DV:(2 * c + h + 1) * DV],
                            scalar=orstd[:, g:g + 1], in1=gate[:, 2 * half + c, h * DV:(h + 1) * DV],
                            op0=ALU.mult, op1=ALU.mult).then_inc(y_done, 1)

        def y_low(dve, cell, half):
            prev = cell.shifted(-1)
            bk, _ = t_turn(cell, f"y{half}")
            dve.wait_ge(yt_hi_done, prev.count(2, half + 1))
            nc.vector.tensor_tensor(yt_lo[:, half, :, :, :].rearrange("p c h t -> p (c h t)"), TB[bk][:],
                                    yt_hi[:, half, :, :, :].rearrange("p c h t -> p (c h t)").bitcast(F32),
                                    ALU.subtract).then_inc(yt_lo_done, 1)

        def kept(dve, cell, c, summed, done, dst, src, rows_own):
            dve.wait_ge(summed, cell.count(CH - 1, c + 1))
            nc.vector.tensor_tensor(dst, src, rows_own, ALU.mult).then_inc(done, 1)

        def add_rows(dve, cell, c):
            prev = cell.shifted(-1)
            bk, _ = p_turn(cell, f"wo{c}")
            a = acc[:, prev.batch * CH + c, :]
            dve.wait_ge(rows, prev.count(CH, c + 1))
            nc.vector.tensor_tensor(a, PB[bk][:], a, ALU.add).then_inc(added, 1)

        def low_rows(dve, J):
            for i in (7, 8):
                dve.wait_ge(wo_hi_done, J * 2 + (i - 6))
                nc.vector.scalar_tensor_tensor(out=part(i, 1), in0=raw[:, i % 3, :], scalar=gn[:, 1:2],
                                               in1=part(i, 0).bitcast(F32), op0=ALU.mult,
                                               op1=ALU.subtract).then_inc(wo_lo_done, 1)

        def cell_vector(dve, cell, wo_J=None, last=False):
            nxt = cell.shifted(1)
            if not first(cell):
                y_vector(dve, cell.shifted(-1))

            def keep_keys(c):
                kept(dve, cell, c, hk_summed, hk_kept, hk[:, c, :], XB[:, 0:P], own[:, :, 0:M])

            gate_vector(dve, cell, 0)
            keep_keys(0)
            gate_vector(dve, cell, 1)
            keep_keys(1)
            masked(dve, cell, 0, scores, scores_masked)
            masked(dve, cell, 1, scores, scores_masked)
            keep_keys(2)
            if not first(cell):
                y_low(dve, cell, 0)
                y_low(dve, cell, 1)
            flat = ok[:].rearrange("p c h m -> p (c h m)")
            groups = ok[:].rearrange("p c h m -> p (c h) m")
            dve.wait_ge(ok_summed, cell.count(1, 1))
            dve.wait_ge(rz_tok_done, cell.count(1, 1))
            nc.vector.tensor_tensor(flat, OB[:], rz_tok[:].rearrange("p c n -> p (c n)"),
                                    ALU.mult).then_inc(ok_scaled, 1)
            dve.wait_ge(ok_scaled, cell.count(1, 1))
            nc.vector.tensor_reduce(top[:], groups, AX_X, ALU.max).then_inc(top_done, 1)
            if not first(cell):
                add_rows(dve, cell, 0)
            dve.wait_ge(top_done, cell.count(1, 1))
            nc.vector.tensor_tensor(groups, groups,
                                    top[:].rearrange("p (g a) -> p g a", a=1).broadcast_to([P, 2 * CH, M]),
                                    ALU.subtract).then_inc(ok_less_top, 1)
            if not first(cell):
                add_rows(dve, cell, 1)
            dve.wait_ge(exp_done, cell.count(1, 1))
            nc.vector.tensor_tensor(pz[:].rearrange("p c h m -> p (c h m)"), flat,
                                    rz_tok[:].rearrange("p c n -> p (c n)"), ALU.mult).then_inc(pz_done, 1)
            if not first(cell):
                add_rows(dve, cell, 2)
            nc.vector.tensor_reduce(esum[:], groups, AX_X, ALU.add).then_inc(esum_done, 1)
            dve.wait_ge(esum_done, cell.count(1, 1))
            nc.vector.scalar_tensor_tensor(out=esq[:], in0=esum[:], scalar=EPS, in1=esum[:], op0=ALU.mult,
                                           op1=ALU.mult).then_inc(esq_done, 1)
            if not first(cell):
                add_rows(dve, cell, 3)
            for c in range(CH - 1):
                kept(dve, cell, c, hv_summed, hv_kept, hv[:, c, :], XB[:, P:P + VW],
                     own[:].rearrange("p h n -> p (h n)"))
                if c == 1:
                    bk, _ = t_turn(cell, "pz")
                    dve.wait_ge(pz_t_done, cell.count(1, 1))
                    nc.vector.tensor_tensor(bd_lo[0:M, 0, :], TB[bk][0:M, :], bd_hi[0:M, 0, :].bitcast(F32),
                                            ALU.subtract)
                    nc.vector.tensor_tensor(bd_lo[M:P, 1, :], TB[bk][M:P, :], bd_hi[M:P, 1, :].bitcast(F32),
                                            ALU.subtract).then_inc(pz_lo_done, 1)
                if c < 2:
                    gate_vector(dve, cell, c + 2)
            if not last:
                slots_vector(dve, nxt)
                sums_vector(dve, nxt)
            masked(dve, cell, 0, weights, weights_masked)
            masked(dve, cell, 1, weights, weights_masked)
            if not last:
                inverse_vector(dve, nxt)
            if not last:
                queries_low(dve, nxt)
            if wo_J is not None:
                low_rows(dve, wo_J)
            dve.wait_ge(osq_done, cell.count(2 * CH, 2 * CH))
            dve.wait_ge(esq_done, cell.count(1, 1))
            nc.vector.scalar_tensor_tensor(out=ovar[:], in0=osq[:], scalar=1.0 / DV, in1=esq[:], op0=ALU.mult,
                                           op1=ALU.add).then_inc(ovar_done, 1)

        @block.vector
        def _(dve):
            nc.vector.memset(ident[:], 0.0).then_inc(own_done, 1)
            nc.vector.memset(causal[:], 1.0).then_inc(own_done, 1)
            nc.vector.memset(own[:], 0.0).then_inc(own_done, 1)
            nc.vector.memset(bd_hi[:].bitcast(F32), 0.0).then_inc(own_done, 1)
            nc.vector.memset(bd_lo[:].bitcast(F32), 0.0).then_inc(own_done, 1)
            nc.vector.memset(e_tok[:], 0.0).then_inc(own_done, 1)
            dve.wait_ge(own_done, 6)
            nc.vector.memset(own[0:M, 0, :], 1.0).then_inc(own_done, 1)
            nc.vector.memset(own[M:P, 1, :], 1.0).then_inc(own_done, 1)

            def x_low(b):
                for kt in range(KT):
                    g = b * KT + kt
                    dve.wait_ge(xt_hi_done, g + 1)
                    nc.vector.tensor_tensor(xt_lo[b][:, kt, :], XTB[g % 4][:], xt_hi[b][:, kt, :].bitcast(F32),
                                            ALU.subtract).then_inc(xt_lo_done, 1)

            m = Cell(None, 0)
            x_low(0)
            slots_vector(dve, m)
            x_low(1)
            sums_vector(dve, m)
            queries_low(dve, m)
            x_low(2)
            x_low(3)
            inverse_vector(dve, m)
            dve.wait_ge(gn_half, 1)
            low_rows(dve, 0)
            dve.wait_ge(const_done, 2)
            dve.wait_ge(own_done, 8)
            cell_vector(dve, m)
            with dve.Fori(0, PAIRS - 1) as j:
                for b in range(1, B + 1):
                    cell_vector(dve, Cell(j, b), j + 1 if b == 4 else None)
            for b in range(1, B):
                cell_vector(dve, Cell(None, B * (PAIRS - 1) + b), last=b == B - 1)
            tail = Cell(None, CELLS)
            y_vector(dve, tail.shifted(-1))
            y_low(dve, tail, 0)
            y_low(dve, tail, 1)
            for c in range(CH):
                add_rows(dve, tail, c)

        p_read = {"s": (s_clipped, 1, 2), "q": (q_lo_done, 1, 2), "k": (k_done, 1, 2)}
        t_read = {"e": (e_tok_done, 1, 1), "k": (k_tok_done, 1, 1), "rz": (rz_tok_done, 1, 1), "pz": (pz_lo_done, 1, 1)}
        for c in range(CH):
            p_read[f"vg{c}"] = (gate_done, CH, c + 1)
            p_read[f"wo{c}"] = (added, CH, c + 1 - CH)
        for half in range(2):
            t_read[f"y{half}"] = (yt_lo_done, 2, half - 1)

        def wait_read(pe, read, before):
            if before is not None:
                its_cell, use = before
                done, per_cell, k = read[use]
                pe.wait_ge(done, its_cell.count(per_cell, k))

        def split_product(out_, terms, done=None):
            n = len(terms)
            for k, ((lh, ll), (rh, rl)) in enumerate(terms):
                nc.tensor.matmul(out_, lh, rh, start=(k == 0), stop=False)
                nc.tensor.matmul(out_, lh, rl, start=False, stop=False)
                last = nc.tensor.matmul(out_, ll, rh, start=False, stop=(k == n - 1))
            return last if done is None else last.then_inc(done, 1)

        def feature_proj(pe, m, i, done):
            bk, before = p_turn(m.shifted(-1), "sqk"[i])
            wait_read(pe, p_read, before)
            if first(m):
                pe.wait_ge(w_lo_done, i + 1)
            elif m.j is not None and m.b == B:
                pe.wait_ge(w_lo_done, (m.j + 1) * 7 + (i + 1))
            b = m.batch
            split_product(PB[bk][:], [((wsqk_hi[:, i, kt, :], wsqk_lo[:, i, kt, :]),
                                       (xt_hi[b][:, kt, :], xt_lo[b][:, kt, :])) for kt in range(KT)], done)

        def token_proj(pe, cell, c):
            bk, before = p_turn(cell, f"vg{c}")
            wait_read(pe, p_read, before)
            if c == 0 and first(cell):
                pe.wait_ge(w_lo_done, 7)
            if c == 0 and cell.j is not None and cell.b == B:
                pe.wait_ge(w_lo_done, (cell.j + 1) * 7 + 7)
            t = tokens(c)
            b = cell.batch
            split_product(PB[bk][:], [((xt_hi[b][:, kt, t], xt_lo[b][:, kt, t]),
                                       (wvg_hi[:, kt, :], wvg_lo[:, kt, :])) for kt in range(KT)], vg_proj)

        def turned(pe, cell, use, blocks, done):
            bk, before = t_turn(cell, use)
            wait_read(pe, t_read, before)
            for i, blk in enumerate(blocks):
                last = nc.tensor.transpose(TB[bk][:, i * P:(i + 1) * P], blk, ident[:])
            last.then_inc(done, 1)

        def turned_y(pe, cell, half):
            pe.wait_ge(y_done, cell.count(2 * CH, (half - 1) * CH))
            turned(pe, cell, f"y{half}", [y[:, c, h, :] for c in (2 * half, 2 * half + 1) for h in range(2)], y_turned)

        def output_rows(pe, cell, c):
            prev = cell.shifted(-1)
            bk, before = p_turn(cell, f"wo{c}")
            wait_read(pe, p_read, before)
            pe.wait_ge(yt_lo_done, prev.count(2, c // 2 + 1))
            if c == 0:
                if cell.j is not None and cell.b == 1:
                    pe.wait_ge(wo_lo_done, cell.j * 2 + 2)
                elif cell.j is None and cell.b == CELLS - B + 1:
                    pe.wait_ge(wo_lo_done, 2 * PAIRS)
            split_product(PB[bk][:], [((yt_hi[:, c // 2, c % 2, h, :], yt_lo[:, c // 2, c % 2, h, :]),
                                       (wo_hi[:, h, :], wo_lo[:, h, :])) for h in range(2)], rows)

        def pair_blocks(pe, half, done):
            for c in (2 * half, 2 * half + 1):
                t = tokens(c)
                last = split_product(
                    SB[half][:, (c % 2) * 2 * P:(c % 2 + 1) * 2 * P].rearrange("p (h t) -> p h t", h=2),
                    [((lhs_hi[:, t], lhs_lo[:, t]), (bd_hi[:, :, t], bd_lo[:, :, t]))])
            last.then_inc(done, 1)

        def cell_tensor(pe, cell, last=False):
            nxt = cell.shifted(1)
            e = e_t[:, cell.b % 2, :]
            pe.wait_ge(e_done, cell.count(1, 1))
            turned(pe, cell, "e", [e[:, tokens(c)] for c in range(CH)], e_turned)
            pe.wait_ge(k_done, cell.count(1, 1))
            turned(pe, cell, "k", [k_t[:, tokens(c)] for c in range(CH)], k_turned)

            def running_keys(c):
                if c > 0:
                    pe.wait_ge(hk_kept, cell.count(CH - 1, c))
                nc.tensor.matmul(XB[:, 0:P], k_tok[:, c, :], e_tok[:, c, 1:3, :].rearrange("p h m -> p (h m)"),
                                 start=(c == 0), stop=True, skip_group_check=True).then_inc(hk_summed, 1)

            token_proj(pe, cell, 0)
            pe.wait_ge(e_tok_done, cell.count(1, 1))
            pe.wait_ge(k_tok_done, cell.count(1, 1))
            if first(cell):
                pe.wait_ge(xt_lo_done, B * KT)
            running_keys(0)
            token_proj(pe, cell, 1)
            running_keys(1)
            pe.wait_ge(q_done, cell.count(1, 1))
            if not first(cell):
                pe.wait_ge(y_done, cell.count(2 * CH, 0))
            pe.wait_ge(q_lo_done, cell.count(1, 1))
            pe.wait_ge(k_lo_done, cell.count(1, 1))
            pair_blocks(pe, 0, scores)
            pair_blocks(pe, 1, scores)
            running_keys(2)
            pe.wait_ge(rz_done, cell.count(1, 1))
            turned(pe, cell, "rz", [rz_t[:, tokens(c)] for c in range(CH)], rz_turned)
            if not first(cell):
                turned_y(pe, cell, 0)
            for c in range(CH):
                if c == 2 and not first(cell):
                    turned_y(pe, cell, 1)
                o = OB[:, c * P:(c + 1) * P]
                if c > 0:
                    pe.wait_ge(hk_kept, cell.count(CH - 1, c))
                    nc.tensor.matmul(o, q_t[:, tokens(c)], hk[:, c - 1, :], start=True, stop=False)
                pe.wait_ge(scores_masked, cell.count(2, c // 2 + 1))
                nc.tensor.matmul(o.rearrange("p (h m) -> p h m", h=2), w_t[:, c, 0, :], e_tok[:, c, 1:4:2, :],
                                 start=(c == 0), stop=False)
                mm = nc.tensor.matmul(o.rearrange("p (h m) -> p h m", h=2), w_t[:, c, 1, :], e_tok[:, c, 0:3:2, :],
                                      start=False, stop=True)
            mm.then_inc(ok_summed, 1)
            if not first(cell):
                for c in range(CH):
                    output_rows(pe, cell, c)

            def running_values(c):
                pe.wait_ge(v_done, cell.count(CH, c + 1))
                if c > 0:
                    pe.wait_ge(hv_kept, cell.count(CH - 1, c))
                else:
                    pe.wait_ge(hk_kept, cell.count(CH - 1, CH - 1))
                nc.tensor.matmul(XB[:, P:P + VW], e_tok[:, c, 1:3, :].rearrange("p h m -> p (h m)"), v_tok[:, c, :], start=(c == 0),
                                 stop=True, skip_group_check=True).then_inc(hv_summed, 1)

            running_values(0)
            token_proj(pe, cell, 2)
            running_values(1)
            pe.wait_ge(pz_done, cell.count(1, 1))
            turned(pe, cell, "pz", [pz[:, c, :, :].rearrange("p h m -> p (h m)") for c in range(CH)], pz_turned)
            token_proj(pe, cell, 3)
            running_values(2)
            if not last:
                feature_proj(pe, nxt, 0, s_proj)
            pe.wait_ge(pz_lo_done, cell.count(1, 1))
            pe.wait_ge(e_lo_done, cell.count(1, 1))
            pair_blocks(pe, 0, weights)
            pair_blocks(pe, 1, weights)
            if not last:
                feature_proj(pe, nxt, 1, q_proj)
                feature_proj(pe, nxt, 2, k_proj)
            pe.wait_ge(v_done, cell.count(CH, CH))
            for half in range(2):
                pe.wait_ge(weights_masked, cell.count(2, half + 1))
                for c in (2 * half, 2 * half + 1):
                    o = (OB, SB[0])[half][:, (c % 2) * VW:(c % 2 + 1) * VW]
                    if c > 0:
                        pe.wait_ge(hv_kept, cell.count(CH - 1, c))
                        nc.tensor.matmul(o, pz_t[:, tokens(c)], hv[:, c - 1, :], start=True, stop=False, skip_group_check=True)
                    for h in range(2):
                        mm = nc.tensor.matmul(o[:, h * DV:(h + 1) * DV], w_t[:, c, h, :],
                                              v_tok[:, c, h * DV:(h + 1) * DV],
                                              start=(c == 0), stop=True, skip_group_check=True)
                mm.then_inc(values, 1)

        @block.tensor
        def _(pe):
            pe.wait_ge(const_done, 1)
            m = Cell(None, 0)
            for b in range(B):
                pe.wait_ge(x_in[b], 16)
                for kt in range(KT):
                    g = b * KT + kt
                    if g >= 4:
                        pe.wait_ge(xt_lo_done, g - 3)
                    for c in range(CH):
                        mm = nc.tensor.transpose(XTB[g % 4][:, tokens(c)], acc[:, b * CH + c, kt * P:(kt + 1) * P], ident[:])
                    mm.then_inc(xt_turned, 1)
                if b == 0:
                    pe.wait_ge(xt_lo_done, KT)
                if b < 3:
                    feature_proj(pe, m, b, (s_proj, q_proj, k_proj)[b])
            cell_tensor(pe, m)
            with pe.Fori(0, PAIRS - 1) as j:
                for b in range(1, B + 1):
                    cell_tensor(pe, Cell(j, b))
            for b in range(1, B):
                cell_tensor(pe, Cell(None, B * (PAIRS - 1) + b), last=b == B - 1)
            tail = Cell(None, CELLS)
            turned_y(pe, tail, 0)
            turned_y(pe, tail, 1)
            for c in range(CH):
                output_rows(pe, tail, c)

    return u_raw, v_raw, w1_raw


def experts(nc, acc, ident, raws, raw_sems, b1, W2, b2, out):
    KR = K_EXP * R_EXP
    G = B
    ctx = ExitStack()
    with ctx:
        def sb(name, shape, dt=F32):
            return ctx.enter_context(nc.sbuf_tensor(name, shape, dt))

        def sem(name):
            return ctx.enter_context(nc.semaphore(name))

        u_raw, v_raw, w1_raw = raws
        u_in, v_in, w1_in = raw_sems
        sb("loaded", [P, 3, KT * D])
        w1_hi, w1_lo = sb("w1_hi", [P, KT, D], F32R), sb("w1_lo", [P, KT, D], F32R)
        vt_hi, vt_lo = sb("vt_hi", [P, KT, KR], F32R), sb("vt_lo", [P, KT, KR], F32R)
        ut_hi, ut_lo = sb("ut_hi", [P, KT, D], F32R), sb("ut_lo", [P, KT, D], F32R)
        w2_pad = sb("w2_pad", [P, KT, P])
        b1_col = sb("b1_col", [P, KT])
        b2_row = sb("b2_row", [P, K_EXP])
        xs = sb("xs", [P, CH, D])
        x1t_hi, x1t_lo = sb("x1t_hi", [P, KT, T], F32R), sb("x1t_lo", [P, KT, T], F32R)
        ht = sb("ht", [P, KT, T])
        w = sb("w", [P, CH, K_EXP, R_EXP])
        wt_hi, wt_lo = sb("wt_hi", [P, CH, KT, P], F32R), sb("wt_lo", [P, CH, KT, P], F32R)
        alpha = sb("alpha", [P, CH, K_EXP])
        a_top, a_sum = sb("a_top", [P, CH]), sb("a_sum", [P, CH])
        st1, st2 = sb("st1", [P, CH, 6]), sb("st2", [P, CH, 6])
        mv1, mv2 = sb("mv1", [P, CH, 2]), sb("mv2", [P, CH, 2])
        va1, va2 = sb("va1", [P, CH]), sb("va2", [P, CH])
        rs1, rs2 = sb("rs1", [P, CH]), sb("rs2", [P, CH])
        half = sb("half", [P, CH])

        AB = [ctx.enter_context(nc.psum_tensor(f"a{i}", [P, BANK], F32)) for i in range(4)]
        LB = ctx.enter_context(nc.psum_tensor("l", [P, BANK], F32))
        XT = [ctx.enter_context(nc.psum_tensor(f"xt{i}", [P, BANK], F32)) for i in range(2)]
        WT = [ctx.enter_context(nc.psum_tensor("wt", [P, BANK], F32)), LB]

        small_in, w2_in, out_sent = sem("small_in"), sem("w2_in"), sem("out_sent")
        zeroed, half_set = sem("zeroed"), sem("half_set")
        prep_turned, prep_hi, prep_lo = sem("prep_turned"), sem("prep_hi"), sem("prep_lo")
        stats1, moments1, var1, rstd1, x1_done = sem("stats1"), sem("moments1"), sem("var1"), sem("rstd1"), sem("x1_done")
        stats2, moments2, var2, rstd2, x2_done = sem("stats2"), sem("moments2"), sem("var2"), sem("rstd2"), sem("x2_done")
        xs_done, x_turned, x_hi, x_lo = sem("xs_done"), sem("x_turned"), sem("x_hi"), sem("x_lo")
        h_proj, h_done, logits, vx = sem("h_proj"), sem("h_done"), sem("logits"), sem("vx")
        a_biased, a_topped, a_less_top, a_exp = sem("a_biased"), sem("a_topped"), sem("a_less_top"), sem("a_exp")
        a_summed, a_inverse, alpha_done = sem("a_summed"), sem("a_inverse"), sem("alpha_done")
        w_done, w_turned, w_hi, w_lo = sem("w_done"), sem("w_turned"), sem("w_hi"), sem("w_lo")
        rows, added = sem("f_rows"), sem("f_added")

        block = ctx.enter_context(nc.Block())

        def tile(g, t):
            if isinstance(g, int):
                return acc[:, g * CH + t, :]
            return acc[:, bass.ds(g * CH + t, 1), :].rearrange("p a d -> p (a d)")

        @block.sync
        def _(sp):
            for n in range(KT):
                sp.dma_start(b1_col[:, n:n + 1],
                             b1[n * P:(n + 1) * P].rearrange("(p a) -> p a", a=1)).then_inc(small_in, 16)
            sp.dma_start(b2_row[:], b2.partition_broadcast(P)).then_inc(small_in, 16)
            sp.wait_ge(zeroed, 1)
            sp.dma_start(w2_pad[:, :, 0:K_EXP], W2.rearrange("(a p) n -> p a n", p=P)).then_inc(w2_in, 16)
            ov = out.rearrange("b (t p) d -> p b t d", p=P)
            for g in range(G):
                for t in range(CH):
                    sp.wait_ge(x2_done, g * CH + t + 1)
                    sp.dma_start(ov[:, g, t, :], acc[:, g * CH + t, :]).then_inc(out_sent, 16)
            sp.wait_ge(out_sent, 16 * G * CH)

        @block.gpsimd
        def _(pool):
            nc.gpsimd.memset(half[:], -0.5).then_inc(half_set, 1)
            pool.wait_ge(half_set, 1)
            for g in range(G + 1):
                if g < G:
                    pool.wait_ge(var1, g + 1)
                    nc.gpsimd.tensor_tensor(rs1[:], va1[:], half[:], ALU.pow).then_inc(rstd1, 1)
                if g > 0:
                    pool.wait_ge(var2, g)
                    nc.gpsimd.tensor_tensor(rs2[:], va2[:], half[:], ALU.pow).then_inc(rstd2, 1)

        PE_TURNS = [("w", 0), ("w", 1), ("x", 0), ("x", 1), ("w", 2), ("x", 2), ("w", 3), ("x", 3)]

        def prep_part(n, which):
            m, k = divmod(n, KT)
            return ((vt_hi, vt_lo), (ut_hi, ut_lo), (w1_hi, w1_lo))[m][which][:, k, :]

        def prep_source(n):
            return AB[n % 4][:] if n < 2 * KT else w1_raw[:, n - 2 * KT, :]

        @block.scalar
        def _(act):
            def copy_x1(g):
                for t in range(CH):
                    act.wait_ge(x1_done, g * CH + t + 1)
                    nc.scalar.activation(xs[:, t, :], tile(g, t), ACT.Copy).then_inc(xs_done, 1)

            def x_high(g, kt):
                act.wait_ge(x_turned, g * KT + kt + 1)
                nc.scalar.activation(x1t_hi[:, kt, :], XT[kt % 2][:], ACT.Copy).then_inc(x_hi, 1)

            for n in range(3 * KT):
                if n < 2 * KT:
                    act.wait_ge(prep_turned, n + 1)
                elif n == 2 * KT:
                    act.wait_ge(w1_in, 16)
                nc.scalar.activation(prep_part(n, 0), prep_source(n), ACT.Copy).then_inc(prep_hi, 1)
            act.wait_ge(small_in, 16 * (KT + 1))
            copy_x1(0)
            for kt in range(KT):
                x_high(0, kt)

            def group(g, last):
                for n in range(KT):
                    act.wait_ge(h_proj, g * KT + n + 1)
                    nc.scalar.activation(ht[:, n, :], AB[n][:], ACT.Relu, bias=b1_col[:, n:n + 1]).then_inc(h_done, 1)
                act.wait_ge(a_less_top, g + 1)
                nc.scalar.activation(alpha[:], alpha[:], ACT.Exp).then_inc(a_exp, 1)
                if not last:
                    copy_x1(g + 1)
                for kind, k in PE_TURNS:
                    if kind == "w":
                        act.wait_ge(w_turned, g * CH + k + 1)
                        nc.scalar.activation(wt_hi[:, k, :, :].rearrange("p a t -> p (a t)"),
                                             WT[k % 2][:], ACT.Copy).then_inc(w_hi, 1)
                    elif not last:
                        x_high(g + 1, k)

            for g in range(G):
                group(g, g == G - 1)

        @block.vector
        def _(dve):
            def norm1(g):
                for t in range(CH):
                    nc.vector.bn_stats(out=st1[:, t, :], in_=tile(g, t)).then_inc(stats1, 1)
                    dve.wait_ge(stats1, g * CH + t + 1)
                    nc.vector.bn_aggr(out=mv1[:, t, :], in_=st1[:, t, :]).then_inc(moments1, 1)
                dve.wait_ge(moments1, (g + 1) * CH)
                nc.vector.tensor_scalar(va1[:], mv1[:, :, 1], EPS, None, ALU.add).then_inc(var1, 1)
                dve.wait_ge(rstd1, g + 1)
                for t in range(CH):
                    nc.vector.tensor_scalar(tile(g, t), tile(g, t), mv1[:, t, 0:1], rs1[:, t:t + 1],
                                            ALU.subtract, ALU.mult).then_inc(x1_done, 1)

            def x_low(g, kt):
                dve.wait_ge(x_hi, g * KT + kt + 1)
                nc.vector.tensor_tensor(x1t_lo[:, kt, :], XT[kt % 2][:],
                                        x1t_hi[:, kt, :].bitcast(F32), ALU.subtract).then_inc(x_lo, 1)

            nc.vector.memset(w2_pad[:], 0.0).then_inc(zeroed, 1)
            norm1(0)
            for n in range(3 * KT):
                dve.wait_ge(prep_hi, n + 1)
                nc.vector.tensor_tensor(prep_part(n, 1), prep_source(n), prep_part(n, 0).bitcast(F32),
                                        ALU.subtract).then_inc(prep_lo, 1)
            for kt in range(KT):
                x_low(0, kt)

            def add_tile(g, t):
                dve.wait_ge(rows, g * CH + t + 1)
                nc.vector.tensor_tensor(tile(g, t), AB[t][:], tile(g, t), ALU.add).then_inc(added, 1)
                dve.wait_ge(added, g * CH + t + 1)
                nc.vector.bn_stats(out=st2[:, t, :], in_=tile(g, t)).then_inc(stats2, 1)
                dve.wait_ge(stats2, g * CH + t + 1)
                nc.vector.bn_aggr(out=mv2[:, t, :], in_=st2[:, t, :]).then_inc(moments2, 1)

            def norm2(g):
                dve.wait_ge(rstd2, g + 1)
                for t in range(CH):
                    nc.vector.tensor_scalar(tile(g, t), tile(g, t), mv2[:, t, 0:1], rs2[:, t:t + 1],
                                            ALU.subtract, ALU.mult).then_inc(x2_done, 1)

            def group(g, last):
                if not last:
                    norm1(g + 1)
                if g > 0:
                    norm2(g - 1)
                dve.wait_ge(logits, g + 1)
                nc.vector.tensor_tensor(alpha[:], LB[:].rearrange("p (t n) -> p t n", t=CH)[:, :, 0:K_EXP],
                                        b2_row[:].rearrange("p (a k) -> p a k", a=1).broadcast_to([P, CH, K_EXP]),
                                        ALU.add).then_inc(a_biased, 1)
                dve.wait_ge(a_biased, g + 1)
                nc.vector.tensor_reduce(a_top[:], alpha[:], AX_X, ALU.max).then_inc(a_topped, 1)
                dve.wait_ge(a_topped, g + 1)
                nc.vector.tensor_tensor(alpha[:], alpha[:],
                                        a_top[:].rearrange("p (t a) -> p t a", a=1).broadcast_to([P, CH, K_EXP]),
                                        ALU.subtract).then_inc(a_less_top, 1)
                dve.wait_ge(a_exp, g + 1)
                nc.vector.tensor_reduce(a_sum[:], alpha[:], AX_X, ALU.add).then_inc(a_summed, 1)
                dve.wait_ge(a_summed, g + 1)
                nc.vector.reciprocal(a_sum[:], a_sum[:]).then_inc(a_inverse, 1)
                dve.wait_ge(a_inverse, g + 1)
                nc.vector.tensor_tensor(alpha[:], alpha[:],
                                        a_sum[:].rearrange("p (t a) -> p t a", a=1).broadcast_to([P, CH, K_EXP]),
                                        ALU.mult).then_inc(alpha_done, 1)
                dve.wait_ge(alpha_done, g + 1)
                for t in range(CH):
                    dve.wait_ge(vx, g * CH + t + 1)
                    nc.vector.tensor_tensor(
                        w[:, t, :, :], AB[t][:].rearrange("p (k r) -> p k r", k=K_EXP),
                        alpha[:, t, :].rearrange("p (k a) -> p k a", a=1).broadcast_to([P, K_EXP, R_EXP]),
                        ALU.mult).then_inc(w_done, 1)
                adds = 0
                for kind, k in PE_TURNS:
                    if kind == "w":
                        dve.wait_ge(w_hi, g * CH + k + 1)
                        nc.vector.tensor_tensor(wt_lo[:, k, :, :].rearrange("p a t -> p (a t)"), WT[k % 2][:],
                                                wt_hi[:, k, :, :].rearrange("p a t -> p (a t)").bitcast(F32),
                                                ALU.subtract).then_inc(w_lo, 1)
                    elif not last:
                        x_low(g + 1, k)
                for t in range(CH):
                    add_tile(g, t)
                dve.wait_ge(moments2, (g + 1) * CH)
                nc.vector.tensor_scalar(va2[:], mv2[:, :, 1], EPS, None, ALU.add).then_inc(var2, 1)

            for g in range(G):
                group(g, g == G - 1)
            norm2(G - 1)

        @block.tensor
        def _(pe):
            def split_product(out_, terms, done):
                n = len(terms)
                for k, ((lh, ll), (rh, rl)) in enumerate(terms):
                    nc.tensor.matmul(out_, lh, rh, start=(k == 0), stop=False)
                    nc.tensor.matmul(out_, lh, rl, start=False, stop=False)
                    last = nc.tensor.matmul(out_, ll, rh, start=False, stop=(k == n - 1))
                last.then_inc(done, 1)

            def tokens(t):
                return slice(t * P, (t + 1) * P)

            def blocks(bank_, blks, done):
                for i, blk in enumerate(blks):
                    mm = nc.tensor.transpose(bank_[:, tokens(i)], blk, ident[:])
                mm.then_inc(done, 1)

            for n in range(2 * KT):
                m, k = divmod(n, KT)
                if k == 0:
                    pe.wait_ge((v_in, u_in)[m], (16, 16 * KT)[m])
                if n >= 4:
                    pe.wait_ge(prep_lo, n - 3)
                if m == 0:
                    blks = [v_raw[:, i, k * P:(k + 1) * P] for i in range(KT)]
                else:
                    blks = [u_raw[:, i, 2 * k:2 * k + 2, :].rearrange("p k r -> p (k r)") for i in range(KT)]
                blocks(AB[n % 4], blks, prep_turned)

            def x_turn(g, kt):
                if g * KT + kt >= 2:
                    pe.wait_ge(x_lo, g * KT + kt - 1)
                pe.wait_ge(xs_done, (g + 1) * CH)
                blocks(XT[kt % 2], [xs[:, t, kt * P:(kt + 1) * P] for t in range(CH)], x_turned)

            for kt in range(KT):
                x_turn(0, kt)
            pe.wait_ge(prep_lo, 3 * KT)
            pe.wait_ge(w2_in, 16)

            def group(g, last):
                pe.wait_ge(x_lo, (g + 1) * KT)
                for n in range(KT):
                    if g > 0:
                        pe.wait_ge(added, (g - 1) * CH + n + 1)
                    split_product(AB[n][:], [((w1_hi[:, kt, tokens(n)], w1_lo[:, kt, tokens(n)]),
                                              (x1t_hi[:, kt, :], x1t_lo[:, kt, :])) for kt in range(KT)], h_proj)

                def vx_tile(t):
                    pe.wait_ge(h_done, g * KT + t + 1)
                    split_product(AB[t][:], [((x1t_hi[:, kt, tokens(t)], x1t_lo[:, kt, tokens(t)]),
                                              (vt_hi[:, kt, :], vt_lo[:, kt, :])) for kt in range(KT)], vx)

                vx_tile(0)
                pe.wait_ge(h_done, (g + 1) * KT)
                for t in range(CH):
                    for n in range(KT):
                        mm = nc.tensor.matmul(LB[:, tokens(t)], ht[:, n, tokens(t)], w2_pad[:, n, :],
                                              start=(n == 0), stop=(n == KT - 1))
                mm.then_inc(logits, 1)
                for t in range(1, CH):
                    vx_tile(t)

                def turn_one(i):
                    kind, k = PE_TURNS[i]
                    if kind == "w":
                        pe.wait_ge(w_done, g * CH + k + 1)
                        if g * CH + k >= 2:
                            pe.wait_ge(w_lo, g * CH + k - 1)
                        blocks(WT[k % 2], [w[:, k, 2 * n:2 * n + 2, :].rearrange("p k r -> p (k r)") for n in range(KT)],
                               w_turned)
                    elif not last:
                        x_turn(g + 1, k)

                def out_tile(t):
                    pe.wait_ge(w_lo, g * CH + t + 1)
                    split_product(AB[t][:], [((wt_hi[:, t, n, :], wt_lo[:, t, n, :]),
                                              (ut_hi[:, n, :], ut_lo[:, n, :])) for n in range(KT)], rows)

                for i in range(4):
                    turn_one(i)
                out_tile(0)
                turn_one(4)
                turn_one(5)
                out_tile(1)
                turn_one(6)
                turn_one(7)
                out_tile(2)
                out_tile(3)

            for g in range(G):
                group(g, g == G - 1)


_INS = ["L0_attn_hidden_states", "L0_attn_Wq", "L0_attn_Wk", "L0_attn_Wv", "L0_attn_Wg", "L0_attn_Ws", "L0_attn_Wo",
        "L0_attn_g_norm_weight", "L0_ffn_U", "L0_ffn_V", "L0_ffn_W1", "L0_ffn_b1", "L0_ffn_W2", "L0_ffn_b2"]
_OUT = (B, T, D)


def kernel(**inputs):
    import numpy as _np
    import concourse.bacc as _bacc
    from concourse import mybir as _mybir
    from concourse.bass_utils import run_bass_kernel_spmd as _run

    nc = _bacc.Bacc("TRN2", target_bir_lowering=False, num_devices=1)
    arrays, args = {}, []
    for name in _INS:
        a = _np.ascontiguousarray(inputs[name])
        arrays[f"in_{name}"] = a
        args.append(nc.dram_tensor(f"in_{name}", a.shape, _mybir.dt.from_np(a.dtype), kind="ExternalInput").ap())
    args.append(nc.dram_tensor("out", _OUT, _mybir.dt.float32, kind="ExternalOutput").ap())
    build(nc, *args)
    r = _run(nc, [arrays], core_ids=[0])
    return r.results[0]["out"]
```

```python
from contextlib import ExitStack

import concourse.bass as bass
from concourse import mybir
from concourse.alu_op_type import AluOpType as ALU

ACT = mybir.ActivationFunctionType
F32 = mybir.dt.float32
F32R = mybir.dt.float32r
AX_X = mybir.AxisListType.X

P = 128
BANK = 512

B, T, D = 4, 512, 512
H, DK, DV, M = 16, 64, 128, 64
R_KEEP, K_EXP, R_EXP = 128, 8, 64
CLAMP = 32.0
EPS = 1e-5

KT = D // P
PAIRS = H // 2
CH = T // P
CELLS = PAIRS * B
VW = 2 * DV
NT = B * CH
KR = K_EXP * R_EXP


class Cell:

    def __init__(self, j, b):
        self.j, self.b = j, b

    def shifted(self, by):
        return Cell(self.j, self.b + by)

    @property
    def batch(self):
        return self.b % B

    def count(self, per_cell, k=0):
        fixed = per_cell * self.b + k
        return fixed if self.j is None else self.j * (per_cell * B) + fixed


P_USES = ["vg0", "vg1", "wo0", "wo1", "wo2", "wo3", "vg2", "vg3", "s", "q", "k"]
T_USES = ["e", "k", "rz", "y0", "y1", "pz"]


def turn(cell, use, uses, start):
    def order(number):
        if number == 0:
            return [u for u in uses if u[:2] != "wo" and u[0] != "y"]
        if number == CELLS:
            return [u for u in uses if u[:2] == "wo" or u[0] == "y"]
        if number == CELLS - 1 and uses is P_USES:
            return [u for u in uses if u not in ("s", "q", "k")]
        return uses

    line = [(-1, u) for u in start]
    line += [(n, u) for n in range(cell.b + 1) for u in order(n)]
    at = line.index((cell.b, use))
    n, before = line[at - 2] if at >= 2 else (None, None)
    return at % 2, None if n is None else (cell.shifted(n - cell.b), before)


def p_turn(cell, use):
    return turn(cell, use, P_USES, ["s", "q", "k"])


def t_turn(cell, use):
    return turn(cell, use, T_USES, [])


class Carried:

    def __init__(self, nc, ctx):
        self.nc = nc

        def sb(name, shape, dt=F32):
            return ctx.enter_context(nc.sbuf_tensor(name, shape, dt))

        def sem(name):
            return ctx.enter_context(nc.semaphore(name))

        self.acc = sb("acc", [P, NT, D])
        self.ident = sb("ident", [P, P])
        self.minus_half = sb("minus_half", [P, 2 * CH])
        self.b1_col = sb("b1_col", [P, KT])
        self.b2_row = sb("b2_row", [P, K_EXP])
        self.st1, self.mv1 = sb("st1", [P, CH, 6]), sb("mv1", [P, CH, 2])
        self.va1, self.rs1 = sb("va1", [P, CH]), sb("rs1", [P, CH])
        self.v_in, self.u_in, self.w1_in, self.small_in = sem("v_in"), sem("u_in"), sem("w1_in"), sem("small_in")
        self.prep_turned, self.prep_hi, self.prep_lo = sem("prep_turned"), sem("prep_hi"), sem("prep_lo")
        self.w1_hi_done, self.w1_lo_done = sem("w1_hi_done"), sem("w1_lo_done")
        self.stats1, self.moments1, self.var1 = sem("stats1"), sem("moments1"), sem("var1")
        self.rstd1, self.x1_done = sem("rstd1"), sem("x1_done")
        self.x_turned, self.x_hi, self.x_lo = sem("x_turned"), sem("x_hi"), sem("x_lo")
        with ExitStack() as early:
            def later(name, shape, dt=F32):
                return early.enter_context(nc.sbuf_tensor(name, shape, dt))

            self.v_raw = later("v_raw", [P, KT, D])
            self.u_raw = later("u_raw", [P, KT, K_EXP, R_EXP])
            self.w1_raw = later("w1_raw", [P, KT, D])
            self.vt = later("vt_hi", [P, KT, KR], F32R), later("vt_lo", [P, KT, KR], F32R)
            self.ut = later("ut_hi", [P, KT, D], F32R), later("ut_lo", [P, KT, D], F32R)
            self.w1 = later("w1_hi", [P, KT, D], F32R), later("w1_lo", [P, KT, D], F32R)
            self.x1t = later("x1t_hi", [P, KT, T], F32R), later("x1t_lo", [P, KT, T], F32R)
        self.later_tiles = 11

    def tile(self, g, t):
        return self.acc[:, g * CH + t, :]

    def prep_part(self, n, which):
        return (self.vt, self.ut)[n // KT][which][:, n % KT, :]

    def prep_turn(self, pe, n, bank_):
        if n % KT == 0:
            pe.wait_ge((self.v_in, self.u_in)[n // KT], (16, 16 * KT)[n // KT])
        k = n % KT
        if n < KT:
            blocks = [self.v_raw[:, i, k * P:(k + 1) * P] for i in range(KT)]
        else:
            blocks = [self.u_raw[:, i, 2 * k:2 * k + 2, :].rearrange("p k r -> p (k r)") for i in range(KT)]
        for i, blk in enumerate(blocks):
            last = self.nc.tensor.transpose(bank_[:, i * P:(i + 1) * P], blk, self.ident[:])
        last.then_inc(self.prep_turned, 1)

    def prep_high(self, act, n, bank_):
        act.wait_ge(self.prep_turned, n + 1)
        self.nc.scalar.activation(self.prep_part(n, 0), bank_[:], ACT.Copy).then_inc(self.prep_hi, 1)

    def prep_low(self, dve, n, bank_):
        dve.wait_ge(self.prep_hi, n + 1)
        self.nc.vector.tensor_tensor(self.prep_part(n, 1), bank_[:], self.prep_part(n, 0).bitcast(F32),
                                     ALU.subtract).then_inc(self.prep_lo, 1)

    def w1_high(self, act, kt):
        if kt == 0:
            act.wait_ge(self.w1_in, 16)
        self.nc.scalar.activation(self.w1[0][:, kt, :], self.w1_raw[:, kt, :], ACT.Copy).then_inc(self.w1_hi_done, 1)

    def w1_low(self, pool, kt):
        pool.wait_ge(self.w1_hi_done, kt + 1)
        self.nc.gpsimd.tensor_tensor(self.w1[1][:, kt, :], self.w1_raw[:, kt, :],
                                     self.w1[0][:, kt, :].bitcast(F32), ALU.subtract).then_inc(self.w1_lo_done, 1)

    def norm1_stats(self, dve, g):
        for t in range(CH):
            self.nc.vector.bn_stats(out=self.st1[:, t, :], in_=self.tile(g, t)).then_inc(self.stats1, 1)
            dve.wait_ge(self.stats1, g * CH + t + 1)
            self.nc.vector.bn_aggr(out=self.mv1[:, t, :], in_=self.st1[:, t, :]).then_inc(self.moments1, 1)
        dve.wait_ge(self.moments1, (g + 1) * CH)
        self.nc.vector.tensor_scalar(self.va1[:], self.mv1[:, :, 1], EPS, None, ALU.add).then_inc(self.var1, 1)

    def norm1_rstd(self, pool, g):
        pool.wait_ge(self.var1, g + 1)
        self.nc.gpsimd.tensor_tensor(self.rs1[:], self.va1[:], self.minus_half[:, 0:CH],
                                     ALU.pow).then_inc(self.rstd1, 1)

    def norm1_apply(self, dve, g):
        dve.wait_ge(self.rstd1, g + 1)
        for t in range(CH):
            self.nc.vector.tensor_scalar(self.tile(g, t), self.tile(g, t), self.mv1[:, t, 0:1], self.rs1[:, t:t + 1],
                                         ALU.subtract, ALU.mult).then_inc(self.x1_done, 1)

    def x_turn(self, pe, g, kt, bank_):
        pe.wait_ge(self.x1_done, (g + 1) * CH)
        for t in range(CH):
            last = self.nc.tensor.transpose(bank_[:, t * P:(t + 1) * P], self.tile(g, t)[:, kt * P:(kt + 1) * P],
                                            self.ident[:])
        last.then_inc(self.x_turned, 1)

    def x_high(self, act, g, kt, bank_):
        act.wait_ge(self.x_turned, g * KT + kt + 1)
        self.nc.scalar.activation(self.x1t[0][:, kt, :], bank_[:], ACT.Copy).then_inc(self.x_hi, 1)

    def x_low(self, dve, g, kt, bank_):
        dve.wait_ge(self.x_hi, g * KT + kt + 1)
        self.nc.vector.tensor_tensor(self.x1t[1][:, kt, :], bank_[:], self.x1t[0][:, kt, :].bitcast(F32),
                                     ALU.subtract).then_inc(self.x_lo, 1)


def build(nc, x, Wq, Wk, Wv, Wg, Ws, Wo, g_norm, U, V, W1, b1, W2, b2, out):
    with ExitStack() as whole:
        car = Carried(nc, whole)
        attention(nc, car, x, Wq, Wk, Wv, Wg, Ws, Wo, g_norm, U, V, W1, b1, b2)
        experts(nc, car, W2, out)


def attention(nc, car, x, Wq, Wk, Wv, Wg, Ws, Wo, g_norm, U, V, W1, b1, b2):
    acc, ident, minus_half = car.acc, car.ident, car.minus_half
    ctx = ExitStack()
    with ctx:
        def sb(name, shape, dt=F32):
            return ctx.enter_context(nc.sbuf_tensor(name, shape, dt))

        def bank(name):
            return ctx.enter_context(nc.psum_tensor(name, [P, BANK], F32))

        def sem(name):
            return ctx.enter_context(nc.semaphore(name))

        xt_hi, xt_lo = [], []
        for b in range(B):
            xt_hi.append(sb(f"xt_hi{b}", [P, KT, T], F32R))
            xt_lo.append(sb(f"xt_lo{b}", [P, KT, T], F32R))
        wsqk_hi = sb("wsqk_hi", [P, 3, KT, P], F32R)
        wsqk_lo = sb("wsqk_lo", [P, 3, KT, P], F32R)
        wvg_hi = sb("wvg_hi", [P, KT, 2 * VW], F32R)
        wvg_lo = sb("wvg_lo", [P, KT, 2 * VW], F32R)
        wo_hi = sb("wo_hi", [P, 2, D], F32R)
        wo_lo = sb("wo_lo", [P, 2, D], F32R)
        raw = sb("raw", [P, 3, BANK])
        e_t = sb("e_t", [P, 2, T])
        rz_t = sb("rz_t", [P, T])
        bd_hi, bd_lo = sb("bd_hi", [P, 2, T], F32R), sb("bd_lo", [P, 2, T], F32R)
        lhs_hi, lhs_lo = sb("lhs_hi", [P, T], F32R), sb("lhs_lo", [P, T], F32R)
        k_t = sb("k_t", [P, T])
        e_tok = sb("e_tok", [P, CH, 4, M])
        with ExitStack() as early:
            k_tok = early.enter_context(nc.sbuf_tensor("k_tok", [P, CH, P], F32))
            rz_tok = early.enter_context(nc.sbuf_tensor("rz_tok", [P, CH, P], F32))
            hk = early.enter_context(nc.sbuf_tensor("hk", [P, CH - 1, P], F32))
        pz_t_hi, pz_t_lo = sb("pz_t_hi", [P, CH, P], F32R), sb("pz_t_lo", [P, CH, P], F32R)
        hv_lo, hv_hi = sb("hv_lo", [P, CH - 1, VW], F32R), sb("hv_hi", [P, CH - 1, VW], F32R)
        ok = sb("ok", [P, CH, 2, M])
        pz = sb("pz", [P, CH, 2, M])
        v_tok = sb("v_tok", [P, CH, VW])
        gate = sb("gate", [P, CH, VW])
        th = sb("th", [P, 2, VW])
        with ExitStack() as early:
            v_hi = early.enter_context(nc.sbuf_tensor("v_hi", [P, CH - 1, VW], F32R))
            v_lo = early.enter_context(nc.sbuf_tensor("v_lo", [P, CH - 1, VW], F32R))
            e_tok_hi = early.enter_context(nc.sbuf_tensor("e_tok_hi", [P, CH - 1, P], F32R))
            e_tok_lo = early.enter_context(nc.sbuf_tensor("e_tok_lo", [P, CH - 1, P], F32R))
        y = sb("y", [P, CH, 2, DV])
        w_t = sb("w_t", [P, CH, 2, P])
        q_t = sb("q_t", [P, T])
        yt_hi = sb("yt_hi", [P, 2, 2, 2, P], F32R)
        yt_lo = sb("yt_lo", [P, 2, 2, 2, P], F32R)
        causal = sb("causal", [P, P])
        own = sb("own", [P, 2, DV])
        gn = sb("gn", [P, 2])
        top = sb("top", [P, 2 * CH])
        esum = sb("esum", [P, 2 * CH])
        esq = sb("esq", [P, 2 * CH])
        osq = sb("osq", [P, 2 * CH])
        ovar = sb("ovar", [P, 2 * CH])
        orstd = sb("orstd", [P, 2 * CH])

        PB = [bank("p0"), bank("p1")]
        TB = [bank("t0"), bank("t1")]
        SB = [bank("s0"), bank("s1")]
        OB = bank("o")
        XB = bank("xb")
        XTB = [SB[0], SB[1], OB, XB]

        x_in = [sem(f"x_in{b}") for b in range(B)]
        raw_in = [sem(f"raw_in{i}") for i in range(3)]
        gn_in = sem("gn_in")
        w_hi_done = sem("w_hi_done")
        w_lo_done = sem("w_lo_done")
        wo_hi_done = sem("wo_hi_done")
        wo_lo_done = sem("wo_lo_done")
        const_done = sem("const_done")
        own_done = sem("own_done")
        gn_half = sem("gn_half")
        xt_turned = sem("xt_turned")
        xt_hi_done = sem("xt_hi_done")
        xt_lo_done = sem("xt_lo_done")
        s_proj, q_proj, k_proj, vg_proj = sem("s_proj"), sem("q_proj"), sem("k_proj"), sem("vg_proj")
        e_turned, k_turned, rz_turned = sem("e_turned"), sem("k_turned"), sem("rz_turned")
        y_turned, pz_turned = sem("y_turned"), sem("pz_turned")
        scores = sem("scores")
        hk_summed, ok_summed, hv_summed = sem("hk_summed"), sem("ok_summed"), sem("hv_summed")
        weights, values, rows = sem("weights"), sem("values"), sem("rows")
        s_clipped, e_done, z_done, rz_done = sem("s_clipped"), sem("e_done"), sem("z_done"), sem("rz_done")
        q_done, k_done, v_done, th_done, gate_done = (
            sem("q_done"), sem("k_done"), sem("v_done"), sem("th_done"), sem("gate_done"))
        e_tok_done, k_tok_done, rz_tok_done = sem("e_tok_done"), sem("k_tok_done"), sem("rz_tok_done")
        scores_masked, weights_masked = sem("scores_masked"), sem("weights_masked")
        hk_kept, hv_hi_done, hv_kept = sem("hk_kept"), sem("hv_hi_done"), sem("hv_kept")
        ok_scaled, top_done, ok_less_top, exp_done = (
            sem("ok_scaled"), sem("top_done"), sem("ok_less_top"), sem("exp_done"))
        pz_done, esum_done, esq_done = sem("pz_done"), sem("esum_done"), sem("esq_done")
        pz_t_done, pz_lo_done = sem("pz_t_done"), sem("pz_lo_done")
        q_lo_done, k_lo_done = sem("q_lo_done"), sem("k_lo_done")
        e_hi_done, e_lo_done = sem("e_hi_done"), sem("e_lo_done")
        e_tok_hi_done, e_tok_lo_done = sem("e_tok_hi_done"), sem("e_tok_lo_done")
        v_hi_done, v_lo_done = sem("v_hi_done"), sem("v_lo_done")
        osq_done, ovar_done, orstd_done = sem("osq_done"), sem("ovar_done"), sem("orstd_done")
        y_done, yt_hi_done, yt_lo_done = sem("y_done"), sem("yt_hi_done"), sem("yt_lo_done")
        added = sem("added")

        def tokens(c):
            return slice(c * P, (c + 1) * P)

        def load_piece(sp, J, name, i):
            slot = raw[:, i % 3, :]
            if name == "sqk":
                w = (Ws, Wq, Wk)[i]
                src = w.rearrange("(k p) n -> p k n", p=P)[:, :, bass.ds(J * P, P)]
                sp.dma_start(slot.rearrange("p (k n) -> p k n", k=KT), src).then_inc(raw_in[i % 3], 16)
            elif name == "vg":
                kt = i - 3
                for half, w in ((0, Wv), (1, Wg)):
                    src = w[kt * P:(kt + 1) * P, bass.ds(J * VW, VW)]
                    sp.dma_start(slot[:, half * VW:(half + 1) * VW], src).then_inc(raw_in[i % 3], 16)
            else:
                h = i - 7
                src = Wo[bass.ds(J * VW + h * DV, DV), :]
                sp.dma_start(slot, src).then_inc(raw_in[i % 3], 16)

        LANDED = {0: (0, 1), 3: (0, 3), 6: (0, 5), 1: (1, 1), 4: (1, 3), 7: (1, 4), 2: (2, 1), 5: (2, 3), 8: (2, 4)}
        PER_PAIR = (5, 4, 4)

        def wait_landed(eng, J, i):
            slot, k = LANDED[i]
            eng.wait_ge(raw_in[slot], J * (16 * PER_PAIR[slot]) + 16 * k)

        def name_of(i):
            return "sqk" if i < 3 else "vg" if i < 7 else "wo"

        def part(i, which):
            if i < 3:
                return (wsqk_hi, wsqk_lo)[which][:, i, :, :].rearrange("p k n -> p (k n)")
            if i < 7:
                return (wvg_hi, wvg_lo)[which][:, i - 3, :]
            return (wo_hi, wo_lo)[which][:, i - 7, :]

        bank_v0, bank_v1 = [PB[p_turn(Cell(None, CELLS - 1), use)[0]] for use in ("vg2", "vg3")]
        PREP = [bank_v0, bank_v1, TB[0], TB[1], SB[1], XB, bank_v0, bank_v1]
        X1 = [SB[1], XB, OB, SB[0]]

        def first(cell):
            return cell.j is None and cell.b == 0

        block = ctx.enter_context(nc.Block())

        @block.sync
        def _(sp):
            sp.dma_start(gn[:, 0:1], g_norm.rearrange("(p a) -> p a", a=1)).then_inc(gn_in, 16)
            xv = x.rearrange("b (n p) d -> b p n d", p=P)
            sp.dma_start(acc[:, 0:CH, :], xv[0]).then_inc(x_in[0], 16)
            for i in range(3):
                load_piece(sp, 0, name_of(i), i)
            for b in range(1, B - 1):
                sp.dma_start(acc[:, b * CH:(b + 1) * CH, :], xv[b]).then_inc(x_in[b], 16)
            for i in range(3, 9):
                sp.wait_ge(w_lo_done, i - 2)
                load_piece(sp, 0, name_of(i), i)
                if i == 5:
                    sp.dma_start(acc[:, (B - 1) * CH:B * CH, :], xv[B - 1]).then_inc(x_in[B - 1], 16)
            with sp.Fori(1, PAIRS) as J:
                for i in range(9):
                    if i == 0:
                        sp.wait_ge(w_lo_done, J * 7)
                    elif i < 3:
                        sp.wait_ge(wo_lo_done, J * 2 + (i - 2))
                    else:
                        sp.wait_ge(w_lo_done, J * 7 + (i - 2))
                    load_piece(sp, J, name_of(i), i)
            sp.wait_ge(vg_proj, CH * (CELLS - B + 1))
            sp.dma_start(car.v_raw[:], V.rearrange("k r d -> (k r) d").rearrange("(a p) d -> p a d", p=P)).then_inc(car.v_in, 16)
            for kt in range(KT):
                sp.dma_start(car.u_raw[:, kt, :, :],
                             U.rearrange("k (a p) r -> a p k r", p=P)[kt]).then_inc(car.u_in, 16)
            sp.wait_ge(vg_proj, CH * (CELLS - B + 2))
            sp.dma_start(car.w1_raw[:], W1.rearrange("(a p) n -> p a n", p=P)).then_inc(car.w1_in, 16)
            for n in range(KT):
                sp.dma_start(car.b1_col[:, n:n + 1],
                             b1[n * P:(n + 1) * P].rearrange("(p a) -> p a", a=1)).then_inc(car.small_in, 16)
            sp.dma_start(car.b2_row[:], b2.partition_broadcast(P)).then_inc(car.small_in, 16)

        def split_low(pool, J, i):
            pool.wait_ge(w_hi_done, J * 7 + (i + 1))
            nc.gpsimd.tensor_tensor(part(i, 1), raw[:, i % 3, :], part(i, 0).bitcast(F32),
                                    ALU.subtract).then_inc(w_lo_done, 1)

        def keys_low(pool, m):
            pool.wait_ge(k_done, m.count(1, 1))
            nc.gpsimd.tensor_tensor(lhs_lo[:], k_t[:], lhs_hi[:].bitcast(F32), ALU.subtract).then_inc(k_lo_done, 1)

        def cell_gpsimd(pool, cell, J=None, last=False):
            if J is not None:
                for i in range(3):
                    split_low(pool, J, i)
            if last:
                car.norm1_rstd(pool, 0)
            pool.wait_ge(e_hi_done, cell.count(1, 1))
            nc.gpsimd.tensor_tensor(lhs_lo[:], e_t[:, cell.b % 2, :], lhs_hi[:].bitcast(F32),
                                    ALU.subtract).then_inc(e_lo_done, 1)
            pool.wait_ge(e_tok_hi_done, cell.count(1, 1))
            nc.gpsimd.tensor_tensor(e_tok_lo[:].rearrange("p c (h m) -> p c h m", h=2), e_tok[:, 0:CH - 1, 1:3, :],
                                    e_tok_hi[:].rearrange("p c (h m) -> p c h m", h=2).bitcast(F32),
                                    ALU.subtract).then_inc(e_tok_lo_done, 1)
            for c in range(CH - 1):
                pool.wait_ge(v_hi_done, cell.count(CH - 1, c + 1))
                nc.gpsimd.tensor_tensor(v_lo[:, c, :], v_tok[:, c, :], v_hi[:, c, :].bitcast(F32),
                                        ALU.subtract).then_inc(v_lo_done, 1)
            if J is not None:
                for i in range(3, 7):
                    split_low(pool, J, i)
            if not last:
                keys_low(pool, cell.shifted(1))
            pool.wait_ge(ovar_done, cell.count(1, 1))
            nc.gpsimd.tensor_tensor(orstd[:], ovar[:], minus_half[:], ALU.pow).then_inc(orstd_done, 1)

        @block.gpsimd
        def _(pool):
            pool.wait_ge(own_done, 2)
            nc.gpsimd.affine_select(out=ident[:], in_=ident[:], compare_op=ALU.not_equal, fill=1.0, base=0,
                                    pattern=[[-1, P]], channel_multiplier=1).then_inc(const_done, 1)
            nc.gpsimd.affine_select(out=causal[:], in_=causal[:], compare_op=ALU.is_ge, fill=0.0, base=0,
                                    pattern=[[1, P]], channel_multiplier=-1).then_inc(const_done, 1)
            nc.gpsimd.memset(minus_half[:], -0.5).then_inc(const_done, 1)
            for i in range(7):
                split_low(pool, 0, i)
            pool.wait_ge(const_done, 3)
            keys_low(pool, Cell(None, 0))
            cell_gpsimd(pool, Cell(None, 0))
            with pool.Fori(0, PAIRS - 1) as j:
                for b in range(1, B + 1):
                    cell_gpsimd(pool, Cell(j, b), j + 1 if b == 3 else None)
            for b in range(1, B):
                cell_gpsimd(pool, Cell(None, B * (PAIRS - 1) + b), last=b == B - 1)
            for kt in range(KT):
                car.w1_low(pool, kt)

        def split_high(act, J, i, release):
            wait_landed(act, J, i)
            if release is not None:
                act.wait_ge(*release)
            if i < 7:
                nc.scalar.activation(part(i, 0), raw[:, i % 3, :], ACT.Copy).then_inc(w_hi_done, 1)
            else:
                nc.scalar.activation(part(i, 0), raw[:, i % 3, :], ACT.Copy,
                                     scale=gn[:, 1:2]).then_inc(wo_hi_done, 1)

        def slots_scalar(act, m):
            act.wait_ge(s_clipped, m.count(1, 1))
            e = e_t[:, m.b % 2, :]
            nc.scalar.activation(e, e, ACT.Exp).then_inc(e_done, 1)

        def queries_scalar(act, m):
            bk, _ = p_turn(m.shifted(-1), "q")
            ps = PB[bk]
            act.wait_ge(q_proj, m.count(1, 1))
            scale = float(DK) ** -0.5
            nc.scalar.activation(q_t[:], ps[:], ACT.Copy, scale=scale)
            nc.scalar.activation(bd_hi[0:DK, 0, :], ps[0:DK, :], ACT.Copy, scale=scale)
            nc.scalar.activation(bd_hi[DK:P, 1, :], ps[DK:P, :], ACT.Copy, scale=scale).then_inc(q_done, 1)

        def keys_scalar(act, m):
            bk, _ = p_turn(m.shifted(-1), "k")
            act.wait_ge(k_proj, m.count(1, 1))
            nc.scalar.activation(k_t[:], PB[bk][:], ACT.Copy)
            nc.scalar.activation(lhs_hi[:], PB[bk][:], ACT.Copy).then_inc(k_done, 1)

        def values_scalar(act, cell, c):
            bk, _ = p_turn(cell, f"vg{c}")
            act.wait_ge(vg_proj, cell.count(CH, c + 1))
            nc.scalar.activation(v_tok[:, c, :], PB[bk][:, 0:VW], ACT.Copy).then_inc(v_done, 1)
            if c >= 2 or not first(cell):
                act.wait_ge(gate_done, cell.count(CH, c - 1))
            nc.scalar.activation(th[:, c % 2, :], PB[bk][:, VW:2 * VW], ACT.Tanh,
                                 scale=0.5).then_inc(th_done, 1)

        def values_high(act, cell, c):
            act.wait_ge(v_done, cell.count(CH, c + 1))
            nc.scalar.activation(v_hi[:, c, :], v_tok[:, c, :], ACT.Copy).then_inc(v_hi_done, 1)

        def y_high(act, cell, half):
            prev = cell.shifted(-1)
            bk, _ = t_turn(cell, f"y{half}")
            act.wait_ge(y_turned, prev.count(2, half + 1))
            nc.scalar.activation(yt_hi[:, half, :, :, :].rearrange("p c h t -> p (c h t)"), TB[bk][:],
                                 ACT.Copy).then_inc(yt_hi_done, 1)

        def cell_scalar(act, cell, J=None, wo_J=None, last=False):
            nxt = cell.shifted(1)
            bk, _ = t_turn(cell, "e")
            act.wait_ge(e_turned, cell.count(1, 1))
            nc.scalar.activation(e_tok[:, :, 1:3, :], TB[bk][:].rearrange("p (c h m) -> p c h m", c=CH, h=2),
                                 ACT.Copy).then_inc(e_tok_done, 1)
            bk, _ = t_turn(cell, "k")
            act.wait_ge(k_turned, cell.count(1, 1))
            nc.scalar.activation(k_tok[:].rearrange("p c n -> p (c n)"), TB[bk][:], ACT.Copy).then_inc(k_tok_done, 1)
            if J is not None:
                for i, used in ((0, s_proj), (1, q_proj), (2, k_proj)):
                    split_high(act, J, i, (used, J * B))
            values_scalar(act, cell, 0)
            values_scalar(act, cell, 1)
            bk, _ = t_turn(cell, "rz")
            act.wait_ge(rz_turned, cell.count(1, 1))
            nc.scalar.activation(rz_tok[:].rearrange("p c n -> p (c n)"), TB[bk][:], ACT.Copy).then_inc(rz_tok_done, 1)
            act.wait_ge(scores, cell.count(2, 2))
            nc.scalar.activation(lhs_hi[:], e_t[:, cell.b % 2, :], ACT.Copy).then_inc(e_hi_done, 1)
            if not first(cell):
                y_high(act, cell, 0)
                y_high(act, cell, 1)
            act.wait_ge(ok_summed, cell.count(1, 1))
            nc.scalar.activation(e_tok_hi[:].rearrange("p c (h m) -> p c h m", h=2), e_tok[:, 0:CH - 1, 1:3, :],
                                 ACT.Copy).then_inc(e_tok_hi_done, 1)
            values_high(act, cell, 0)
            values_high(act, cell, 1)
            act.wait_ge(ok_less_top, cell.count(1, 1))
            flat = ok[:].rearrange("p c h m -> p (c h m)")
            nc.scalar.activation(flat, flat, ACT.Exp).then_inc(exp_done, 1)
            values_scalar(act, cell, 2)
            values_high(act, cell, 2)
            bk, _ = t_turn(cell, "pz")
            act.wait_ge(pz_turned, cell.count(1, 1))
            nc.scalar.activation(pz_t_hi[:].rearrange("p c t -> p (c t)"), TB[bk][:], ACT.Copy)
            nc.scalar.activation(bd_hi[0:M, 0, :], TB[bk][0:M, :], ACT.Copy)
            nc.scalar.activation(bd_hi[M:P, 1, :], TB[bk][M:P, :], ACT.Copy).then_inc(pz_t_done, 1)
            values_scalar(act, cell, 3)
            if J is not None:
                for i in range(3, 6):
                    split_high(act, J, i, (vg_proj, J * (B * CH)))
            if not last:
                slots_scalar(act, nxt)
                queries_scalar(act, nxt)
            if J is not None:
                split_high(act, J, 6, (vg_proj, J * (B * CH)))
            if not last:
                keys_scalar(act, nxt)
            if wo_J is not None:
                for i in (7, 8):
                    split_high(act, wo_J, i, (rows, wo_J * (B * CH)))
            if last:
                for n in range(KT):
                    car.prep_high(act, n, PREP[n])
                for kt in range(KT - 1):
                    car.w1_high(act, kt)
            for half in range(2):
                ps = (OB, SB[0])[half]
                act.wait_ge(values, cell.count(2, half + 1))
                for c in range(2):
                    for h in range(2):
                        g = (2 * half + c) * 2 + h
                        nc.scalar.activation(y[:, 2 * half + c, h, :], ps[:, (2 * c + h) * DV:(2 * c + h + 1) * DV],
                                             ACT.Square, accum_out=osq[:, g:g + 1]).then_inc(osq_done, 1)

        @block.scalar
        def _(act):
            act.wait_ge(gn_in, 16)
            nc.scalar.activation(gn[:, 1:2], gn[:, 0:1], ACT.Copy, scale=0.5).then_inc(gn_half, 1)

            def x_high(b):
                for kt in range(KT):
                    g = b * KT + kt
                    act.wait_ge(xt_turned, g + 1)
                    nc.scalar.activation(xt_hi[b][:, kt, :], XTB[g % 4][:], ACT.Copy).then_inc(xt_hi_done, 1)

            split_high(act, 0, 0, None)
            x_high(0)
            split_high(act, 0, 1, None)
            split_high(act, 0, 2, None)
            slots_scalar(act, Cell(None, 0))
            split_high(act, 0, 3, None)
            x_high(1)
            split_high(act, 0, 4, None)
            queries_scalar(act, Cell(None, 0))
            split_high(act, 0, 5, None)
            split_high(act, 0, 6, None)
            x_high(2)
            keys_scalar(act, Cell(None, 0))
            x_high(3)
            act.wait_ge(gn_half, 1)
            for i in (7, 8):
                split_high(act, 0, i, None)
            cell_scalar(act, Cell(None, 0))
            with act.Fori(0, PAIRS - 1) as j:
                for b in range(1, B + 1):
                    cell_scalar(act, Cell(j, b), j + 1 if b == 3 else None, j + 1 if b == 4 else None)
            for b in range(1, B):
                cell_scalar(act, Cell(None, B * (PAIRS - 1) + b), last=b == B - 1)
            for n in range(KT, 2 * KT):
                car.prep_high(act, n, PREP[n])
            car.w1_high(act, KT - 1)
            for kt in (0, 1):
                car.x_high(act, 0, kt, X1[kt])
            y_high(act, Cell(None, CELLS), 0)
            y_high(act, Cell(None, CELLS), 1)
            for kt in (2, 3):
                car.x_high(act, 0, kt, X1[kt])

        def slots_vector(dve, m):
            bk, _ = p_turn(m.shifted(-1), "s")
            dve.wait_ge(s_proj, m.count(1, 1))
            nc.vector.tensor_scalar(e_t[:, m.b % 2, :], PB[bk][:], -CLAMP, CLAMP, ALU.max,
                                    ALU.min).then_inc(s_clipped, 1)

        def sums_vector(dve, m):
            dve.wait_ge(e_done, m.count(1, 1))
            e = e_t[:, m.b % 2, :]
            nc.vector.tensor_tensor_scan(rz_t[:], e, e, 0.0, ALU.add, ALU.bypass).then_inc(z_done, 1)

        def inverse_vector(dve, m):
            dve.wait_ge(z_done, m.count(1, 1))
            nc.vector.reciprocal(rz_t[:], rz_t[:]).then_inc(rz_done, 1)

        def queries_low(dve, m):
            bk, _ = p_turn(m.shifted(-1), "q")
            dve.wait_ge(q_done, m.count(1, 1))
            for h, own_rows in enumerate((slice(0, DK), slice(DK, P))):
                low = nc.vector.scalar_tensor_tensor(out=bd_lo[own_rows, h, :], in0=PB[bk][own_rows, :],
                                                     scalar=float(DK) ** -0.5,
                                                     in1=bd_hi[own_rows, h, :].bitcast(F32), op0=ALU.mult,
                                                     op1=ALU.subtract)
            low.then_inc(q_lo_done, 1)

        def masked(dve, cell, half, ready, done):
            dve.wait_ge(ready, cell.count(2, half + 1))
            nc.vector.tensor_tensor(
                w_t[:, 2 * half:2 * half + 2, :, :].rearrange("p c h t -> p (c h) t"),
                SB[half][:].rearrange("p (a t) -> p a t", a=4),
                causal[:].rearrange("p (a t) -> p a t", a=1).broadcast_to([P, 4, P]),
                ALU.mult).then_inc(done, 1)

        def gate_vector(dve, cell, c):
            bk, _ = p_turn(cell, f"vg{c}")
            dve.wait_ge(th_done, cell.count(CH, c + 1))
            if c == 0 and not first(cell):
                dve.wait_ge(y_done, cell.count(2 * CH, 0))
            nc.vector.scalar_tensor_tensor(out=gate[:, c, :], in0=th[:, c % 2, :], scalar=1.0,
                                           in1=PB[bk][:, VW:2 * VW], op0=ALU.add,
                                           op1=ALU.mult).then_inc(gate_done, 1)

        def y_vector(dve, prev):
            dve.wait_ge(orstd_done, prev.count(1, 1))
            dve.wait_ge(gate_done, prev.count(CH, CH))
            for half in range(2):
                ps = (OB, SB[0])[half]
                for c in range(2):
                    for h in range(2):
                        g = (2 * half + c) * 2 + h
                        nc.vector.scalar_tensor_tensor(
                            out=y[:, 2 * half + c, h, :], in0=ps[:, (2 * c + h) * DV:(2 * c + h + 1) * DV],
                            scalar=orstd[:, g:g + 1], in1=gate[:, 2 * half + c, h * DV:(h + 1) * DV],
                            op0=ALU.mult, op1=ALU.mult).then_inc(y_done, 1)

        def y_low(dve, cell, half):
            prev = cell.shifted(-1)
            bk, _ = t_turn(cell, f"y{half}")
            dve.wait_ge(yt_hi_done, prev.count(2, half + 1))
            nc.vector.tensor_tensor(yt_lo[:, half, :, :, :].rearrange("p c h t -> p (c h t)"), TB[bk][:],
                                    yt_hi[:, half, :, :, :].rearrange("p c h t -> p (c h t)").bitcast(F32),
                                    ALU.subtract).then_inc(yt_lo_done, 1)

        def kept(dve, cell, c, summed, done, dst, src, rows_own):
            dve.wait_ge(summed, cell.count(CH - 1, c + 1))
            nc.vector.tensor_tensor(dst, src, rows_own, ALU.mult).then_inc(done, 1)

        def add_rows(dve, cell, c):
            prev = cell.shifted(-1)
            bk, _ = p_turn(cell, f"wo{c}")
            a = acc[:, prev.batch * CH + c, :]
            dve.wait_ge(rows, prev.count(CH, c + 1))
            nc.vector.tensor_tensor(a, PB[bk][:], a, ALU.add).then_inc(added, 1)

        def low_rows(dve, J):
            for i in (7, 8):
                dve.wait_ge(wo_hi_done, J * 2 + (i - 6))
                nc.vector.scalar_tensor_tensor(out=part(i, 1), in0=raw[:, i % 3, :], scalar=gn[:, 1:2],
                                               in1=part(i, 0).bitcast(F32), op0=ALU.mult,
                                               op1=ALU.subtract).then_inc(wo_lo_done, 1)

        def cell_vector(dve, cell, wo_J=None, last=False):
            nxt = cell.shifted(1)
            if not first(cell):
                y_vector(dve, cell.shifted(-1))

            def keep_keys(c):
                kept(dve, cell, c, hk_summed, hk_kept, hk[:, c, :], XB[:, 0:P], own[:, :, 0:M])

            gate_vector(dve, cell, 0)
            keep_keys(0)
            keep_keys(1)
            gate_vector(dve, cell, 1)
            masked(dve, cell, 0, scores, scores_masked)
            masked(dve, cell, 1, scores, scores_masked)
            keep_keys(2)
            if not first(cell):
                y_low(dve, cell, 0)
                y_low(dve, cell, 1)
            flat = ok[:].rearrange("p c h m -> p (c h m)")
            groups = ok[:].rearrange("p c h m -> p (c h) m")
            dve.wait_ge(ok_summed, cell.count(1, 1))
            dve.wait_ge(rz_tok_done, cell.count(1, 1))
            nc.vector.tensor_tensor(flat, OB[:], rz_tok[:].rearrange("p c n -> p (c n)"),
                                    ALU.mult).then_inc(ok_scaled, 1)
            dve.wait_ge(ok_scaled, cell.count(1, 1))
            nc.vector.tensor_reduce(top[:], groups, AX_X, ALU.max).then_inc(top_done, 1)
            if not first(cell):
                add_rows(dve, cell, 0)
            dve.wait_ge(top_done, cell.count(1, 1))
            nc.vector.tensor_tensor(groups, groups,
                                    top[:].rearrange("p (g a) -> p g a", a=1).broadcast_to([P, 2 * CH, M]),
                                    ALU.subtract).then_inc(ok_less_top, 1)
            if not first(cell):
                add_rows(dve, cell, 1)
            dve.wait_ge(exp_done, cell.count(1, 1))
            nc.vector.tensor_tensor(pz[:].rearrange("p c h m -> p (c h m)"), flat,
                                    rz_tok[:].rearrange("p c n -> p (c n)"), ALU.mult).then_inc(pz_done, 1)
            if not first(cell):
                add_rows(dve, cell, 2)
            nc.vector.tensor_reduce(esum[:], groups, AX_X, ALU.add).then_inc(esum_done, 1)
            dve.wait_ge(esum_done, cell.count(1, 1))
            nc.vector.scalar_tensor_tensor(out=esq[:], in0=esum[:], scalar=EPS, in1=esum[:], op0=ALU.mult,
                                           op1=ALU.mult).then_inc(esq_done, 1)
            if not first(cell):
                add_rows(dve, cell, 3)
            for c in range(CH - 1):
                kept(dve, cell, c, hv_summed, hv_hi_done, hv_hi[:, c, :], XB[:, P:P + VW],
                     own[:].rearrange("p h n -> p (h n)"))
                dve.wait_ge(hv_hi_done, cell.count(CH - 1, c + 1))
                for h in range(2):
                    cols = slice(h * DV, (h + 1) * DV)
                    low = nc.vector.scalar_tensor_tensor(out=hv_lo[:, c, cols], in0=XB[:, P + h * DV:P + (h + 1) * DV],
                                                         scalar=own[:, h, 0:1], in1=hv_hi[:, c, cols].bitcast(F32),
                                                         op0=ALU.mult, op1=ALU.subtract)
                low.then_inc(hv_kept, 1)
                if c == 1:
                    bk, _ = t_turn(cell, "pz")
                    dve.wait_ge(pz_t_done, cell.count(1, 1))
                    nc.vector.tensor_tensor(pz_t_lo[:].rearrange("p c t -> p (c t)"), TB[bk][:],
                                            pz_t_hi[:].rearrange("p c t -> p (c t)").bitcast(F32), ALU.subtract)
                    nc.vector.tensor_tensor(bd_lo[0:M, 0, :], TB[bk][0:M, :], bd_hi[0:M, 0, :].bitcast(F32),
                                            ALU.subtract)
                    nc.vector.tensor_tensor(bd_lo[M:P, 1, :], TB[bk][M:P, :], bd_hi[M:P, 1, :].bitcast(F32),
                                            ALU.subtract).then_inc(pz_lo_done, 1)
                if c == 0 and last:
                    car.norm1_apply(dve, 0)
                if c < 2:
                    gate_vector(dve, cell, c + 2)
            if not last:
                slots_vector(dve, nxt)
                sums_vector(dve, nxt)
            masked(dve, cell, 0, weights, weights_masked)
            masked(dve, cell, 1, weights, weights_masked)
            if last:
                for n in range(KT):
                    car.prep_low(dve, n, PREP[n])
            if not last:
                inverse_vector(dve, nxt)
            if not last:
                queries_low(dve, nxt)
            if wo_J is not None:
                low_rows(dve, wo_J)
            if cell.j is None and cell.b == CELLS - 2:
                dve.wait_ge(added, CH * (CELLS - B + 1))
                car.norm1_stats(dve, 0)
            dve.wait_ge(osq_done, cell.count(2 * CH, 2 * CH))
            dve.wait_ge(esq_done, cell.count(1, 1))
            nc.vector.scalar_tensor_tensor(out=ovar[:], in0=osq[:], scalar=1.0 / DV, in1=esq[:], op0=ALU.mult,
                                           op1=ALU.add).then_inc(ovar_done, 1)

        @block.vector
        def _(dve):
            nc.vector.memset(ident[:], 0.0).then_inc(own_done, 1)
            nc.vector.memset(causal[:], 1.0).then_inc(own_done, 1)
            nc.vector.memset(own[:], 0.0).then_inc(own_done, 1)
            nc.vector.memset(bd_hi[:].bitcast(F32), 0.0).then_inc(own_done, 1)
            nc.vector.memset(bd_lo[:].bitcast(F32), 0.0).then_inc(own_done, 1)
            nc.vector.memset(e_tok[:], 0.0).then_inc(own_done, 1)
            dve.wait_ge(own_done, 6)
            nc.vector.memset(own[0:M, 0, :], 1.0).then_inc(own_done, 1)
            nc.vector.memset(own[M:P, 1, :], 1.0).then_inc(own_done, 1)

            def x_low(b):
                for kt in range(KT):
                    g = b * KT + kt
                    dve.wait_ge(xt_hi_done, g + 1)
                    nc.vector.tensor_tensor(xt_lo[b][:, kt, :], XTB[g % 4][:], xt_hi[b][:, kt, :].bitcast(F32),
                                            ALU.subtract).then_inc(xt_lo_done, 1)

            m = Cell(None, 0)
            x_low(0)
            slots_vector(dve, m)
            x_low(1)
            sums_vector(dve, m)
            queries_low(dve, m)
            x_low(2)
            x_low(3)
            inverse_vector(dve, m)
            dve.wait_ge(gn_half, 1)
            low_rows(dve, 0)
            dve.wait_ge(const_done, 2)
            dve.wait_ge(own_done, 8)
            cell_vector(dve, m)
            with dve.Fori(0, PAIRS - 1) as j:
                for b in range(1, B + 1):
                    cell_vector(dve, Cell(j, b), j + 1 if b == 4 else None)
            for b in range(1, B):
                cell_vector(dve, Cell(None, B * (PAIRS - 1) + b), last=b == B - 1)
            tail = Cell(None, CELLS)
            for n in (4, 5):
                car.prep_low(dve, n, PREP[n])
            y_vector(dve, tail.shifted(-1))
            for n in (6, 7):
                car.prep_low(dve, n, PREP[n])
            y_low(dve, tail, 0)
            y_low(dve, tail, 1)
            for kt in range(KT):
                car.x_low(dve, 0, kt, X1[kt])
            for c in range(CH):
                add_rows(dve, tail, c)

        p_read = {"s": (s_clipped, 1, 2), "q": (q_lo_done, 1, 2), "k": (k_done, 1, 2)}
        t_read = {"e": (e_tok_done, 1, 1), "k": (k_tok_done, 1, 1), "rz": (rz_tok_done, 1, 1), "pz": (pz_lo_done, 1, 1)}
        for c in range(CH):
            p_read[f"vg{c}"] = (gate_done, CH, c + 1)
            p_read[f"wo{c}"] = (added, CH, c + 1 - CH)
        for half in range(2):
            t_read[f"y{half}"] = (yt_lo_done, 2, half - 1)

        def wait_read(pe, read, before):
            if before is not None:
                its_cell, use = before
                done, per_cell, k = read[use]
                pe.wait_ge(done, its_cell.count(per_cell, k))

        def split_product(out_, terms, done=None):
            n = len(terms)
            for k, ((lh, ll), (rh, rl)) in enumerate(terms):
                nc.tensor.matmul(out_, lh, rh, start=(k == 0), stop=False)
                nc.tensor.matmul(out_, lh, rl, start=False, stop=False)
                last = nc.tensor.matmul(out_, ll, rh, start=False, stop=(k == n - 1))
            return last if done is None else last.then_inc(done, 1)

        def feature_proj(pe, m, i, done):
            bk, before = p_turn(m.shifted(-1), "sqk"[i])
            wait_read(pe, p_read, before)
            if first(m):
                pe.wait_ge(w_lo_done, i + 1)
            elif m.j is not None and m.b == B:
                pe.wait_ge(w_lo_done, (m.j + 1) * 7 + (i + 1))
            b = m.batch
            split_product(PB[bk][:], [((wsqk_hi[:, i, kt, :], wsqk_lo[:, i, kt, :]),
                                       (xt_hi[b][:, kt, :], xt_lo[b][:, kt, :])) for kt in range(KT)], done)

        def token_proj(pe, cell, c):
            bk, before = p_turn(cell, f"vg{c}")
            wait_read(pe, p_read, before)
            if c == 0 and first(cell):
                pe.wait_ge(w_lo_done, 7)
            if c == 0 and cell.j is not None and cell.b == B:
                pe.wait_ge(w_lo_done, (cell.j + 1) * 7 + 7)
            t = tokens(c)
            b = cell.batch
            split_product(PB[bk][:], [((xt_hi[b][:, kt, t], xt_lo[b][:, kt, t]),
                                       (wvg_hi[:, kt, :], wvg_lo[:, kt, :])) for kt in range(KT)], vg_proj)

        def turned(pe, cell, use, blocks, done):
            bk, before = t_turn(cell, use)
            wait_read(pe, t_read, before)
            for i, blk in enumerate(blocks):
                last = nc.tensor.transpose(TB[bk][:, i * P:(i + 1) * P], blk, ident[:])
            last.then_inc(done, 1)

        def turned_y(pe, cell, half):
            pe.wait_ge(y_done, cell.count(2 * CH, (half - 1) * CH))
            turned(pe, cell, f"y{half}", [y[:, c, h, :] for c in (2 * half, 2 * half + 1) for h in range(2)], y_turned)

        def output_rows(pe, cell, c):
            prev = cell.shifted(-1)
            bk, before = p_turn(cell, f"wo{c}")
            wait_read(pe, p_read, before)
            pe.wait_ge(yt_lo_done, prev.count(2, c // 2 + 1))
            if c == 0:
                if cell.j is not None and cell.b == 1:
                    pe.wait_ge(wo_lo_done, cell.j * 2 + 2)
                elif cell.j is None and cell.b == CELLS - B + 1:
                    pe.wait_ge(wo_lo_done, 2 * PAIRS)
            split_product(PB[bk][:], [((yt_hi[:, c // 2, c % 2, h, :], yt_lo[:, c // 2, c % 2, h, :]),
                                       (wo_hi[:, h, :], wo_lo[:, h, :])) for h in range(2)], rows)

        def pair_blocks(pe, half, done):
            for c in (2 * half, 2 * half + 1):
                t = tokens(c)
                last = split_product(
                    SB[half][:, (c % 2) * 2 * P:(c % 2 + 1) * 2 * P].rearrange("p (h t) -> p h t", h=2),
                    [((lhs_hi[:, t], lhs_lo[:, t]), (bd_hi[:, :, t], bd_lo[:, :, t]))])
            last.then_inc(done, 1)

        def cell_tensor(pe, cell, last=False):
            nxt = cell.shifted(1)
            e = e_t[:, cell.b % 2, :]
            pe.wait_ge(e_done, cell.count(1, 1))
            turned(pe, cell, "e", [e[:, tokens(c)] for c in range(CH)], e_turned)
            pe.wait_ge(k_done, cell.count(1, 1))
            turned(pe, cell, "k", [k_t[:, tokens(c)] for c in range(CH)], k_turned)

            def running_keys(c):
                if c > 0:
                    pe.wait_ge(hk_kept, cell.count(CH - 1, c))
                nc.tensor.matmul(XB[:, 0:P], k_tok[:, c, :], e_tok[:, c, 1:3, :].rearrange("p h m -> p (h m)"),
                                 start=(c == 0), stop=True, skip_group_check=True).then_inc(hk_summed, 1)

            token_proj(pe, cell, 0)
            pe.wait_ge(e_tok_done, cell.count(1, 1))
            pe.wait_ge(k_tok_done, cell.count(1, 1))
            if first(cell):
                pe.wait_ge(xt_lo_done, B * KT)
            running_keys(0)
            token_proj(pe, cell, 1)
            running_keys(1)
            pe.wait_ge(q_done, cell.count(1, 1))
            if not first(cell):
                pe.wait_ge(y_done, cell.count(2 * CH, 0))
            pe.wait_ge(q_lo_done, cell.count(1, 1))
            pe.wait_ge(k_lo_done, cell.count(1, 1))
            pair_blocks(pe, 0, scores)
            pair_blocks(pe, 1, scores)
            running_keys(2)
            pe.wait_ge(rz_done, cell.count(1, 1))
            turned(pe, cell, "rz", [rz_t[:, tokens(c)] for c in range(CH)], rz_turned)
            if not first(cell):
                turned_y(pe, cell, 0)
            for c in range(CH):
                if c == 2 and not first(cell):
                    turned_y(pe, cell, 1)
                o = OB[:, c * P:(c + 1) * P]
                if c > 0:
                    pe.wait_ge(hk_kept, cell.count(CH - 1, c))
                    nc.tensor.matmul(o, q_t[:, tokens(c)], hk[:, c - 1, :], start=True, stop=False)
                pe.wait_ge(scores_masked, cell.count(2, c // 2 + 1))
                nc.tensor.matmul(o.rearrange("p (h m) -> p h m", h=2), w_t[:, c, 0, :], e_tok[:, c, 1:4:2, :],
                                 start=(c == 0), stop=False)
                mm = nc.tensor.matmul(o.rearrange("p (h m) -> p h m", h=2), w_t[:, c, 1, :], e_tok[:, c, 0:3:2, :],
                                      start=False, stop=True)
            mm.then_inc(ok_summed, 1)
            if not first(cell):
                for c in range(CH):
                    output_rows(pe, cell, c)

            def running_values(c):
                pe.wait_ge(v_lo_done, cell.count(CH - 1, c + 1))
                if c > 0:
                    pe.wait_ge(hv_kept, cell.count(CH - 1, c))
                else:
                    pe.wait_ge(e_tok_lo_done, cell.count(1, 1))
                    pe.wait_ge(hk_kept, cell.count(CH - 1, CH - 1))
                parts = ((e_tok_hi, v_hi), (e_tok_hi, v_lo), (e_tok_lo, v_hi))
                for i, (e_part, v_part) in enumerate(parts):
                    mm = nc.tensor.matmul(XB[:, P:P + VW], e_part[:, c, :], v_part[:, c, :],
                                          start=(c == 0 and i == 0), stop=True, skip_group_check=True)
                mm.then_inc(hv_summed, 1)

            running_values(0)
            token_proj(pe, cell, 2)
            running_values(1)
            pe.wait_ge(pz_done, cell.count(1, 1))
            turned(pe, cell, "pz", [pz[:, c, :, :].rearrange("p h m -> p (h m)") for c in range(CH)], pz_turned)
            token_proj(pe, cell, 3)
            running_values(2)
            if not last:
                feature_proj(pe, nxt, 0, s_proj)
            else:
                pe.wait_ge(gate_done, cell.count(CH, CH - 1))
                car.prep_turn(pe, 0, PREP[0])
            pe.wait_ge(pz_lo_done, cell.count(1, 1))
            pe.wait_ge(e_lo_done, cell.count(1, 1))
            pair_blocks(pe, 0, weights)
            pair_blocks(pe, 1, weights)
            if not last:
                feature_proj(pe, nxt, 1, q_proj)
                feature_proj(pe, nxt, 2, k_proj)
            else:
                pe.wait_ge(gate_done, cell.count(CH, CH))
                for n in range(1, KT):
                    car.prep_turn(pe, n, PREP[n])
            pe.wait_ge(v_done, cell.count(CH, CH))
            for half in range(2):
                pe.wait_ge(weights_masked, cell.count(2, half + 1))
                for c in (2 * half, 2 * half + 1):
                    o = (OB, SB[0])[half][:, (c % 2) * VW:(c % 2 + 1) * VW]
                    if c > 0:
                        pe.wait_ge(hv_kept, cell.count(CH - 1, c))
                        split_product(o, [((pz_t_hi[:, c, :], pz_t_lo[:, c, :]),
                                           (hv_hi[:, c - 1, :], hv_lo[:, c - 1, :]))])
                    for h in range(2):
                        mm = nc.tensor.matmul(o[:, h * DV:(h + 1) * DV], w_t[:, c, h, :],
                                              v_tok[:, c, h * DV:(h + 1) * DV],
                                              start=(c == 0), stop=True, skip_group_check=True)
                mm.then_inc(values, 1)

        @block.tensor
        def _(pe):
            pe.wait_ge(const_done, 1)
            m = Cell(None, 0)
            for b in range(B):
                pe.wait_ge(x_in[b], 16)
                for kt in range(KT):
                    g = b * KT + kt
                    if g >= 4:
                        pe.wait_ge(xt_lo_done, g - 3)
                    for c in range(CH):
                        mm = nc.tensor.transpose(XTB[g % 4][:, tokens(c)], acc[:, b * CH + c, kt * P:(kt + 1) * P], ident[:])
                    mm.then_inc(xt_turned, 1)
                if b == 0:
                    pe.wait_ge(xt_lo_done, KT)
                if b < 3:
                    feature_proj(pe, m, b, (s_proj, q_proj, k_proj)[b])
            cell_tensor(pe, m)
            with pe.Fori(0, PAIRS - 1) as j:
                for b in range(1, B + 1):
                    cell_tensor(pe, Cell(j, b))
            for b in range(1, B):
                cell_tensor(pe, Cell(None, B * (PAIRS - 1) + b), last=b == B - 1)
            tail = Cell(None, CELLS)
            for n in range(KT, 2 * KT):
                if n >= 6:
                    pe.wait_ge(car.prep_lo, n - 5)
                car.prep_turn(pe, n, PREP[n])
            for kt in (0, 1):
                pe.wait_ge(car.prep_lo, kt + 5)
                car.x_turn(pe, 0, kt, X1[kt])
            turned_y(pe, tail, 0)
            turned_y(pe, tail, 1)
            for kt in (2, 3):
                pe.wait_ge(y_done, CELLS * 2 * CH)
                car.x_turn(pe, 0, kt, X1[kt])
            pe.wait_ge(car.prep_lo, 2 * KT)
            for c in range(CH):
                output_rows(pe, tail, c)


def experts(nc, car, W2, out):
    G = B
    acc, ident, tile = car.acc, car.ident, car.tile
    (w1_hi, w1_lo), (vt_hi, vt_lo), (ut_hi, ut_lo), (x1t_hi, x1t_lo) = car.w1, car.vt, car.ut, car.x1t
    ctx = ExitStack()
    with ctx:
        def sb(name, shape, dt=F32):
            return ctx.enter_context(nc.sbuf_tensor(name, shape, dt))

        def sem(name):
            return ctx.enter_context(nc.semaphore(name))

        sb("carried", [P, car.later_tiles, KT * D])
        w2_pad = sb("w2_pad", [P, KT, P])
        ht = sb("ht", [P, KT, T])
        w = sb("w", [P, CH, K_EXP, R_EXP])
        wt_hi, wt_lo = sb("wt_hi", [P, CH, KT, P], F32R), sb("wt_lo", [P, CH, KT, P], F32R)
        alpha = sb("alpha", [P, CH, K_EXP])
        a_top, a_sum = sb("a_top", [P, CH]), sb("a_sum", [P, CH])
        st2, mv2 = sb("st2", [P, CH, 6]), sb("mv2", [P, CH, 2])
        va2, rs2 = sb("va2", [P, CH]), sb("rs2", [P, CH])

        AB = [ctx.enter_context(nc.psum_tensor(f"a{i}", [P, BANK], F32)) for i in range(4)]
        LB = ctx.enter_context(nc.psum_tensor("l", [P, BANK], F32))
        XT = [ctx.enter_context(nc.psum_tensor(f"xt{i}", [P, BANK], F32)) for i in range(2)]
        WT = [ctx.enter_context(nc.psum_tensor("wt", [P, BANK], F32)), LB]

        w2_in, out_sent, zeroed = sem("w2_in"), sem("out_sent"), sem("zeroed")
        stats2, moments2, var2, rstd2, x2_done = sem("stats2"), sem("moments2"), sem("var2"), sem("rstd2"), sem("x2_done")
        h_proj, h_done, logits, vx = sem("h_proj"), sem("h_done"), sem("logits"), sem("vx")
        a_biased, a_topped, a_less_top, a_exp = sem("a_biased"), sem("a_topped"), sem("a_less_top"), sem("a_exp")
        a_summed, a_inverse, alpha_done = sem("a_summed"), sem("a_inverse"), sem("alpha_done")
        w_done, w_turned, w_hi, w_lo = sem("w_done"), sem("w_turned"), sem("w_hi"), sem("w_lo")
        rows, added = sem("f_rows"), sem("f_added")

        NORM2 = ([slice(0, CH)], [slice(t, t + 1) for t in range(CH)])

        block = ctx.enter_context(nc.Block())

        @block.sync
        def _(sp):
            sp.wait_ge(zeroed, 1)
            sp.dma_start(w2_pad[:, :, 0:K_EXP], W2.rearrange("(a p) n -> p a n", p=P)).then_inc(w2_in, 16)
            ov = out.rearrange("b (t p) d -> p b t d", p=P)
            for g in range(G):
                for t in range(CH):
                    sp.wait_ge(x2_done, g * CH + t + 1)
                    sp.dma_start(ov[:, g, t, :], acc[:, g * CH + t, :]).then_inc(out_sent, 16)
            sp.wait_ge(out_sent, 16 * G * CH)

        @block.gpsimd
        def _(pool):
            for g in range(1, G + 1):
                if g < G:
                    car.norm1_rstd(pool, g)
                for i, tiles in enumerate(NORM2[g == G]):
                    pool.wait_ge(var2, g + i)
                    nc.gpsimd.tensor_tensor(rs2[:, tiles], va2[:, tiles], car.minus_half[:, tiles],
                                            ALU.pow).then_inc(rstd2, 1)

        PE_TURNS = [("w", 0), ("w", 1), ("x", 0), ("x", 1), ("w", 2), ("x", 2), ("w", 3), ("x", 3)]

        @block.scalar
        def _(act):
            act.wait_ge(car.small_in, 16 * (KT + 1))

            def group(g, last):
                for n in range(KT):
                    act.wait_ge(h_proj, g * KT + n + 1)
                    nc.scalar.activation(ht[:, n, :], AB[n][:], ACT.Relu, bias=car.b1_col[:, n:n + 1]).then_inc(h_done, 1)
                act.wait_ge(a_less_top, g + 1)
                nc.scalar.activation(alpha[:], alpha[:], ACT.Exp).then_inc(a_exp, 1)
                for kind, k in PE_TURNS:
                    if kind == "w":
                        act.wait_ge(w_turned, g * CH + k + 1)
                        nc.scalar.activation(wt_hi[:, k, :, :].rearrange("p a t -> p (a t)"),
                                             WT[k % 2][:], ACT.Copy).then_inc(w_hi, 1)
                    elif not last:
                        car.x_high(act, g + 1, k, XT[k % 2])

            for g in range(G):
                group(g, g == G - 1)

        @block.vector
        def _(dve):
            nc.vector.memset(w2_pad[:], 0.0).then_inc(zeroed, 1)

            def add_tile(g, t):
                dve.wait_ge(rows, g * CH + t + 1)
                nc.vector.tensor_tensor(tile(g, t), AB[t][:], tile(g, t), ALU.add).then_inc(added, 1)
                dve.wait_ge(added, g * CH + t + 1)
                nc.vector.bn_stats(out=st2[:, t, :], in_=tile(g, t)).then_inc(stats2, 1)
                dve.wait_ge(stats2, g * CH + t + 1)
                nc.vector.bn_aggr(out=mv2[:, t, :], in_=st2[:, t, :]).then_inc(moments2, 1)

            def var_plus_eps(g, tiles):
                dve.wait_ge(moments2, g * CH + tiles.stop)
                nc.vector.tensor_scalar(va2[:, tiles], mv2[:, tiles, 1], EPS, None, ALU.add).then_inc(var2, 1)

            def norm2(g, i, tiles):
                dve.wait_ge(rstd2, g + i + 1)
                for t in range(tiles.start, tiles.stop):
                    nc.vector.tensor_scalar(tile(g, t), tile(g, t), mv2[:, t, 0:1], rs2[:, t:t + 1],
                                            ALU.subtract, ALU.mult).then_inc(x2_done, 1)

            def group(g, last):
                if not last:
                    car.norm1_stats(dve, g + 1)
                    car.norm1_apply(dve, g + 1)
                if g > 0:
                    norm2(g - 1, 0, NORM2[0][0])
                dve.wait_ge(logits, g + 1)
                nc.vector.tensor_tensor(alpha[:], LB[:].rearrange("p (t n) -> p t n", t=CH)[:, :, 0:K_EXP],
                                        car.b2_row[:].rearrange("p (a k) -> p a k", a=1).broadcast_to([P, CH, K_EXP]),
                                        ALU.add).then_inc(a_biased, 1)
                dve.wait_ge(a_biased, g + 1)
                nc.vector.tensor_reduce(a_top[:], alpha[:], AX_X, ALU.max).then_inc(a_topped, 1)
                dve.wait_ge(a_topped, g + 1)
                nc.vector.tensor_tensor(alpha[:], alpha[:],
                                        a_top[:].rearrange("p (t a) -> p t a", a=1).broadcast_to([P, CH, K_EXP]),
                                        ALU.subtract).then_inc(a_less_top, 1)
                dve.wait_ge(a_exp, g + 1)
                nc.vector.tensor_reduce(a_sum[:], alpha[:], AX_X, ALU.add).then_inc(a_summed, 1)
                dve.wait_ge(a_summed, g + 1)
                nc.vector.reciprocal(a_sum[:], a_sum[:]).then_inc(a_inverse, 1)
                dve.wait_ge(a_inverse, g + 1)
                nc.vector.tensor_tensor(alpha[:], alpha[:],
                                        a_sum[:].rearrange("p (t a) -> p t a", a=1).broadcast_to([P, CH, K_EXP]),
                                        ALU.mult).then_inc(alpha_done, 1)
                dve.wait_ge(alpha_done, g + 1)

                def weighted(t):
                    dve.wait_ge(vx, g * CH + t + 1)
                    nc.vector.tensor_tensor(
                        w[:, t, :, :], AB[t][:].rearrange("p (k r) -> p k r", k=K_EXP),
                        alpha[:, t, :].rearrange("p (k a) -> p k a", a=1).broadcast_to([P, K_EXP, R_EXP]),
                        ALU.mult).then_inc(w_done, 1)

                def w_low(k):
                    dve.wait_ge(w_hi, g * CH + k + 1)
                    nc.vector.tensor_tensor(wt_lo[:, k, :, :].rearrange("p a t -> p (a t)"), WT[k % 2][:],
                                            wt_hi[:, k, :, :].rearrange("p a t -> p (a t)").bitcast(F32),
                                            ALU.subtract).then_inc(w_lo, 1)

                for t in range(3):
                    weighted(t)
                w_low(0)
                w_low(1)
                weighted(3)
                if last:
                    w_low(2)
                    for t, tiles in enumerate(NORM2[1]):
                        add_tile(g, t)
                        var_plus_eps(g, tiles)
                        if t == 0:
                            w_low(3)
                        else:
                            norm2(g, t - 1, NORM2[1][t - 1])
                    norm2(g, CH - 1, NORM2[1][CH - 1])
                else:
                    for kind, k in PE_TURNS[2:]:
                        if kind == "w":
                            w_low(k)
                        else:
                            car.x_low(dve, g + 1, k, XT[k % 2])
                    for t in range(CH):
                        add_tile(g, t)
                    var_plus_eps(g, NORM2[0][0])

            for g in range(G):
                group(g, g == G - 1)

        @block.tensor
        def _(pe):
            def split_product(out_, terms, done):
                n = len(terms)
                for k, ((lh, ll), (rh, rl)) in enumerate(terms):
                    nc.tensor.matmul(out_, lh, rh, start=(k == 0), stop=False)
                    nc.tensor.matmul(out_, lh, rl, start=False, stop=False)
                    last = nc.tensor.matmul(out_, ll, rh, start=False, stop=(k == n - 1))
                last.then_inc(done, 1)

            def tokens(t):
                return slice(t * P, (t + 1) * P)

            def blocks(bank_, blks, done):
                for i, blk in enumerate(blks):
                    mm = nc.tensor.transpose(bank_[:, tokens(i)], blk, ident[:])
                mm.then_inc(done, 1)

            pe.wait_ge(car.w1_lo_done, KT)

            def group(g, last):
                pe.wait_ge(car.x_lo, (g + 1) * KT)
                for n in range(KT):
                    if g > 0:
                        pe.wait_ge(added, (g - 1) * CH + n + 1)
                    split_product(AB[n][:], [((w1_hi[:, kt, tokens(n)], w1_lo[:, kt, tokens(n)]),
                                              (x1t_hi[:, kt, :], x1t_lo[:, kt, :])) for kt in range(KT)], h_proj)

                def vx_tile(t):
                    pe.wait_ge(h_done, g * KT + t + 1)
                    split_product(AB[t][:], [((x1t_hi[:, kt, tokens(t)], x1t_lo[:, kt, tokens(t)]),
                                              (vt_hi[:, kt, :], vt_lo[:, kt, :])) for kt in range(KT)], vx)

                vx_tile(0)
                if g == 0:
                    pe.wait_ge(w2_in, 16)
                pe.wait_ge(h_done, (g + 1) * KT)
                for t in range(CH):
                    for n in range(KT):
                        mm = nc.tensor.matmul(LB[:, tokens(t)], ht[:, n, tokens(t)], w2_pad[:, n, :],
                                              start=(n == 0), stop=(n == KT - 1))
                mm.then_inc(logits, 1)

                def turn_one(i):
                    kind, k = PE_TURNS[i]
                    if kind == "w":
                        pe.wait_ge(w_done, g * CH + k + 1)
                        if g * CH + k >= 2:
                            pe.wait_ge(w_lo, g * CH + k - 1)
                        blocks(WT[k % 2], [w[:, k, 2 * n:2 * n + 2, :].rearrange("p k r -> p (k r)") for n in range(KT)],
                               w_turned)
                    elif not last:
                        if k >= 2:
                            pe.wait_ge(car.x_lo, (g + 1) * KT + k - 1)
                        car.x_turn(pe, g + 1, k, XT[k % 2])

                def out_tile(t):
                    pe.wait_ge(w_lo, g * CH + t + 1)
                    split_product(AB[t][:], [((wt_hi[:, t, n, :], wt_lo[:, t, n, :]),
                                              (ut_hi[:, n, :], ut_lo[:, n, :])) for n in range(KT)], rows)

                vx_tile(1)
                vx_tile(2)
                turn_one(0)
                turn_one(1)
                vx_tile(3)
                turn_one(2)
                turn_one(3)
                out_tile(0)
                turn_one(4)
                turn_one(5)
                out_tile(1)
                turn_one(6)
                turn_one(7)
                out_tile(2)
                out_tile(3)

            for g in range(G):
                group(g, g == G - 1)


_INS = ["L0_attn_hidden_states", "L0_attn_Wq", "L0_attn_Wk", "L0_attn_Wv", "L0_attn_Wg", "L0_attn_Ws", "L0_attn_Wo",
        "L0_attn_g_norm_weight", "L0_ffn_U", "L0_ffn_V", "L0_ffn_W1", "L0_ffn_b1", "L0_ffn_W2", "L0_ffn_b2"]
_OUT = (B, T, D)


def kernel(**inputs):
    import numpy as _np
    import concourse.bacc as _bacc
    from concourse import mybir as _mybir
    from concourse.bass_utils import run_bass_kernel_spmd as _run

    nc = _bacc.Bacc("TRN2", target_bir_lowering=False, num_devices=1)
    arrays, args = {}, []
    for name in _INS:
        a = _np.ascontiguousarray(inputs[name])
        arrays[f"in_{name}"] = a
        args.append(nc.dram_tensor(f"in_{name}", a.shape, _mybir.dt.from_np(a.dtype), kind="ExternalInput").ap())
    args.append(nc.dram_tensor("out", _OUT, _mybir.dt.float32, kind="ExternalOutput").ap())
    build(nc, *args)
    r = _run(nc, [arrays], core_ids=[0])
    return r.results[0]["out"]
```
